# Optimizing a Trainium2 kernel written in Bass

```python
import numpy as np
import jax
import jax.numpy as jnp

def _softmax(x, axis=-1):
    return jax.nn.softmax(x, axis=axis)

def _gelu(x):
    return jax.nn.gelu(x, approximate=True)

def _silu(x):
    return jax.nn.silu(x)

def _sigmoid(x):
    return jax.nn.sigmoid(x)

def _layernorm(x, axis=-1, eps=1e-05):
    m = jnp.mean(x, axis=axis, keepdims=True)
    v = jnp.var(x, axis=axis, keepdims=True)
    return (x - m) / jnp.sqrt(v + eps)

def _scatter_add(tgt, idx, src, axis=0):
    return tgt.at[idx].add(src)

def _segment_sum(src, seg, n):
    return jax.ops.segment_sum(src, seg, n)
kernel_name = 'mk_adj_resnorm_d1_adj_r2_cd9158'

def setup_inputs(seed: int=0):
    np.random.seed(seed)
    _w = jnp.asarray

    def _rec_inputs():
        import jax
        import jax.numpy as jnp
        _gk = jax.random.key(seed)
        x = -0.0001538 + 1 * jax.random.normal(jax.random.fold_in(_gk, 1), (32, 256, 384), jnp.float32)
        _w = (1.0 + jnp.arange(256, dtype=jnp.float32)) ** (-0.5)
        _w = _w / _w.mean()
        _pij = jnp.clip(0.0625 * _w[:, None] * _w[None, :], 0.0, 1.0)
        _a = jax.random.uniform(jax.random.fold_in(_gk, 2), (32, 256, 256)) < _pij
        _a = jnp.logical_or(_a, jnp.eye(256, dtype=bool))
        adj = _a
        return (x, adj)
    x, adj = _rec_inputs()

    def _L0_gnn_setup():
        import jax, jax.numpy as jnp
        import numpy as np
        B, S, H = (4, 1024, 384)
        NUM_HEADS = 6
        HEAD_SIZE = H // NUM_HEADS
        NEG = -9000000000000000.0

        def _heads(x):
            b, s, _ = x.shape
            return x.reshape(b, s, NUM_HEADS, HEAD_SIZE).transpose(0, 2, 1, 3)
        key = jax.random.key(seed)
        ks = jax.random.split(key, 10)
        seq_inputs = jax.random.normal(ks[0], (B, S, H), dtype=jnp.float32)
        gm = jax.random.randint(ks[1], (B, S, S), 0, 2) > 0
        graph_mask = gm | jnp.eye(S, dtype=bool)[None]
        sc = 1.0 / np.sqrt(H)
        Wq = jax.random.normal(ks[2], (H, H), dtype=jnp.float32) * sc
        bq = jnp.zeros((H,), dtype=jnp.float32)
        Wk = jax.random.normal(ks[3], (H, H), dtype=jnp.float32) * sc
        bk = jnp.zeros((H,), dtype=jnp.float32)
        Wv = jax.random.normal(ks[4], (H, H), dtype=jnp.float32) * sc
        bv = jnp.zeros((H,), dtype=jnp.float32)
        Wf = jax.random.normal(ks[5], (H, H), dtype=jnp.float32) * sc
        bf = jnp.zeros((H,), dtype=jnp.float32)
        return {'seq_inputs': seq_inputs, 'Wq': Wq, 'bq': bq, 'Wk': Wk, 'bk': bk, 'Wv': Wv, 'bv': bv, 'Wf': Wf, 'bf': bf, 'graph_mask': graph_mask}
    _L0_gnn_all = _L0_gnn_setup()
    _L0_gnn_in = {k: v for k, v in _L0_gnn_all.items() if k in ('Wq', 'bq', 'Wk', 'bk', 'Wv', 'bv', 'Wf', 'bf')}
    del _L0_gnn_all
    return {'x': x, 'adj': adj, 'L0_gnn_Wq': _L0_gnn_in['Wq'], 'L0_gnn_bq': _L0_gnn_in['bq'], 'L0_gnn_Wk': _L0_gnn_in['Wk'], 'L0_gnn_bk': _L0_gnn_in['bk'], 'L0_gnn_Wv': _L0_gnn_in['Wv'], 'L0_gnn_bv': _L0_gnn_in['bv'], 'L0_gnn_Wf': _L0_gnn_in['Wf'], 'L0_gnn_bf': _L0_gnn_in['bf']}

def reference(x, adj, L0_gnn_Wq, L0_gnn_bq, L0_gnn_Wk, L0_gnn_bk, L0_gnn_Wv, L0_gnn_bv, L0_gnn_Wf, L0_gnn_bf):
    import jax
    import jax.numpy as jnp

    def _L0_gnn_ref(seq_inputs, Wq, bq, Wk, bk, Wv, bv, Wf, bf, graph_mask):
        import jax, jax.numpy as jnp
        import numpy as np
        B, S, H = (4, 1024, 384)
        NUM_HEADS = 6
        HEAD_SIZE = H // NUM_HEADS
        NEG = -9000000000000000.0

        def _heads(x):
            b, s, _ = x.shape
            return x.reshape(b, s, NUM_HEADS, HEAD_SIZE).transpose(0, 2, 1, 3)
        q = _heads(seq_inputs @ Wq + bq)
        k = _heads(seq_inputs @ Wk + bk)
        v = _heads(seq_inputs @ Wv + bv)
        scores = jnp.einsum('bhqd,bhkd->bhqk', q, k) / np.sqrt(HEAD_SIZE)
        bias = jnp.where(graph_mask, 0.0, NEG)[:, None]
        probs = jax.nn.softmax(scores + bias, axis=-1)
        ctx = jnp.einsum('bhqk,bhkd->bhqd', probs, v)
        ctx = ctx.transpose(0, 2, 1, 3).reshape(seq_inputs.shape[0], seq_inputs.shape[1], H)
        return ctx @ Wf + bf
    x = _layernorm(x + _L0_gnn_ref(x, L0_gnn_Wq, L0_gnn_bq, L0_gnn_Wk, L0_gnn_bk, L0_gnn_Wv, L0_gnn_bv, L0_gnn_Wf, L0_gnn_bf, adj), axis=-1)
    return x

_drawn_inputs = setup_inputs


def setup_inputs(seed=0):
    import zlib

    import numpy as np

    out = dict(_drawn_inputs(seed))
    spreads = {'L0_gnn_bq': (0.0, 0.276),
     'L0_gnn_bk': (0.0, 0.8),
     'L0_gnn_bv': (0.0, 0.1),
     'L0_gnn_bf': (0.0, 0.1)}
    factors = {}
    for name, (base, spread) in spreads.items():
        noise = np.random.default_rng([zlib.crc32(name.encode()), seed]).standard_normal(out[name].shape)
        drawn = base * np.exp(spread * noise) if base else spread * noise
        out[name] = jnp.asarray(drawn.astype(out[name].dtype))
    for name, factor in factors.items():
        out[name] = (out[name] * factor).astype(out[name].dtype)
    return out
```

```python
from contextlib import ExitStack

import numpy as np

import concourse.bass as bass
from concourse import mybir
from concourse.alu_op_type import AluOpType as ALU

F32 = mybir.dt.float32
F32R = mybir.dt.float32r
BF16 = mybir.dt.bfloat16
U8 = mybir.dt.uint8
ACT = mybir.ActivationFunctionType

P = 128
B, T, H = 32, 256, 384
HEADS = 6
D = H // HEADS
C = H // P
J = T // P
SCALE = 1.0 / float(np.sqrt(D))
NEG = -9000000000000000.0
LEAST_START = 3.0e38
EPS = 1e-5
LAST = B + 1
LOOP = (4, 30)


def build(nc, xT, x, adj, wq, wk, wv, wf, bias_cols, bf, eye, out):
    with ExitStack() as ctx:
        def sb(name, shape, dt=F32):
            return ctx.enter_context(nc.sbuf_tensor(name, shape, dt))

        def pair(name, shape, dt=F32):
            return [sb(f"{name}{i}", shape, dt) for i in range(2)]

        def bank(name):
            return ctx.enter_context(nc.psum_tensor(name, [P, 512], F32))

        def sem(name):
            return ctx.enter_context(nc.semaphore(name))

        def sems(name, n):
            return [sem(f"{name}{i}") for i in range(n)]

        w_raw = {k: sb(f"w{k}_raw", [P, C, H]) for k in "qkvf"}
        w_hi = {k: sb(f"w{k}_hi", [P, C, H], F32R) for k in "qkvf"}
        w_lo = {k: sb(f"w{k}_lo", [P, C, H], F32R) for k in "qkvf"}
        ident = sb("ident", [P, P])
        bcol = sb("bcol", [P, 3, C])
        bv_rep = sb("bv_rep", [P, C, P])
        bf_rows = sb("bf_rows", [P, H])
        shift = sb("shift", [P, H])

        xT_raw = pair("xT_raw", [P, C, T])
        xT_hi = pair("xT_hi", [P, C, T], F32R)
        xT_lo = pair("xT_lo", [P, C, T], F32R)
        resid = pair("resid", [P, J, H])
        adj_in = pair("adj_in", [P, J, T], U8)
        mask = pair("mask", [P, J, T], BF16)
        q_stack = pair("q_stack", [P, HEADS, T], F32R)
        k_high2 = pair("k_high2", [P, HEADS, T], F32R)
        k_low0 = pair("k_low0", [P, HEADS, T], F32R)
        v = pair("v", [P, J, H])
        probs = pair("probs", [P, HEADS, J, T])
        least = pair("least", [P, HEADS, J])
        total = pair("total", [P, HEADS, J])
        inv = pair("inv", [P, HEADS, J])
        probsT = sb("probsT", [P, HEADS, J, T])
        ctx_hi = pair("ctx_hi", [P, C, T], F32R)
        ctx_lo = pair("ctx_lo", [P, C, T], F32R)
        y = pair("y", [P, J, H])
        stats = sb("stats", [P, J, 6])
        mean_var = sb("mean_var", [P, J, 2])
        var_eps = sb("var_eps", [P, J])
        minus_half = sb("minus_half", [P, 1])
        rstd = sb("rstd", [P, J])

        bank_a, bank_b = bank("bank_a"), bank("bank_b")
        bank_s = [bank(f"bank_s{i}") for i in range(2)]
        bank_t = [bank(f"bank_t{i}") for i in range(2)]
        bank_c = [bank(f"bank_c{i}") for i in range(2)]
        O_BANK, V_BANK = [bank_b, bank_a], [bank_a, bank_b]

        def q_bank(n, c):
            return bank_a if isinstance(n, int) and n < 3 else [bank_a, bank_b, bank_a][c]

        def k_bank(n, c):
            return bank_b if isinstance(n, int) and n < 3 else [bank_a, bank_b, bank_b][c]

        w_in = {k: sem(f"w{k}_in") for k in "qkvf"}
        w_hi_done, w_lo_done = sem("w_hi_done"), sem("w_lo_done")
        small_in = sem("small_in")
        zeros_done, half_done = sem("zeros_done"), sem("half_done")
        bv_rep_done, shift_mm, shift_done = sem("bv_rep_done"), sem("shift_mm"), sem("shift_done")
        xT_in, x_in, adj_done_in = sems("xT_in", 2), sems("x_in", 2), sems("adj_in_done", 2)
        stored = sems("stored", 2)
        q_mm, k_mm, v_mm = sems("q_mm", C), sems("k_mm", C), sems("v_mm", J)
        s_mm, t_mm = sems("s_mm", HEADS), sems("t_mm", HEADS)
        c_mm, o_mm = sems("c_mm", C), sems("o_mm", J)
        q_hi_done, k_hi_done = sems("q_hi_done", C), sems("k_hi_done", C)
        exp_done, probsT_done = sems("exp_done", HEADS), sems("probsT_done", HEADS)
        ctx_hi_done, v_done = sems("ctx_hi_done", C), sems("v_done", J)
        x_hi_done, mask_done = sem("x_hi_done"), sem("mask_done")
        masked = sems("masked", HEADS)
        inv_done = sems("inv_done", HEADS)
        q_lo_done, k_lo_done, k_twice = sems("q_lo_done", C), sems("k_lo_done", C), sems("k_twice", C)
        ctx_lo_done = sems("ctx_lo_done", C)
        y_done, stats_done, mean_done = sems("y_done", J), sems("stats_done", J), sems("mean_done", J)
        var_done, normed = sems("var_done", J), sems("normed", J)
        x_lo_done, resid_done = sem("x_lo_done"), sem("resid_done")
        probs_done = sems("probs_done", HEADS)
        rstd_done = sems("rstd_done", J)

        def wait(engine, semaphore, batches, apart=False):
            if apart and not isinstance(batches, int):
                engine.wait_ge(small_in, 48)
            if not isinstance(batches, int) or batches > 0:
                engine.wait_ge(semaphore, batches)

        def dmas(n, par):
            return n * 8 + (16 - 8 * par)

        def slots(engine, slot):
            for s in range(-1, LOOP[0]):
                slot(s, s % 2, s + 1)
            with engine.Fori(LOOP[0] + 1, LOOP[1], 2) as odd:
                slot(odd - 1, 0, odd)
                slot(odd, 1, odd + 1)
            for s in range(LOOP[1], LAST + 1):
                slot(s, s % 2, s + 1)

        def within(s, ahead):
            return not isinstance(s, int) or 0 <= s + ahead < B

        block = ctx.enter_context(nc.Block())

        @block.sync
        def _(sp):
            def load_xT(n, par):
                wait(sp, x_lo_done, n - 1, apart=True)
                sp.dma_start(xT_raw[par][:], xT[bass.ds(n, 1)].rearrange("b p c t -> p (b c) t")
                             ).then_inc(xT_in[par], 16)

            def load_adj(n, par):
                wait(sp, mask_done, n - 1, apart=True)
                sp.dma_start(adj_in[par][:], adj[bass.ds(n, 1)].rearrange("b p j t -> p (b j) t")
                             ).then_inc(adj_done_in[par], 16)

            def load_w(k, w):
                sp.dma_start(w_raw[k][:], w.rearrange("(c p) n -> p c n", p=P)).then_inc(w_in[k], 16)

            load_w("q", wq)
            load_xT(0, 0)
            load_w("k", wk)
            sp.dma_start(bcol[:], bias_cols).then_inc(small_in, 16)
            sp.dma_start(ident[:], eye).then_inc(small_in, 16)
            sp.dma_start(bf_rows[:], bf.to_broadcast((P, H))).then_inc(small_in, 16)
            load_adj(0, 0)
            load_w("v", wv)

            def slot(s, par, after):
                if within(s, 2):
                    load_xT(s + 2, par)
                    load_adj(s + 2, par)
                if isinstance(s, int) and s == -1:
                    load_w("f", wf)
                if within(s, 0):
                    wait(sp, y_done[J - 1], s - 1, apart=True)
                    sp.dma_start(resid[par][:], x[bass.ds(s, 1)].rearrange("b (j p) d -> p (b j) d", p=P)
                                 ).then_inc(x_in[par], 16)
                if within(s, -2):
                    wait(sp, normed[J - 1], s - 1, apart=True)
                    sp.dma_start(out[bass.ds(s - 2, 1)].rearrange("b (j p) d -> p (b j) d", p=P), y[par][:]
                                 ).then_inc(stored[par], 16)

            slots(sp, slot)
            for par in range(2):
                sp.wait_ge(stored[par], 16 * (B // 2))

        @block.tensor
        def _(pe):
            def product3(o, hi_hi, hi_lo, lo_hi):
                ops = [f(c) for c in range(C) for f in (hi_hi, hi_lo, lo_hi)]
                for i, (stationary, moving) in enumerate(ops):
                    last = pe.matmul(o, stationary, moving, start=(i == 0), stop=(i == len(ops) - 1))
                return last

            def project(k, bank, c, par):
                cols = slice(c * P, (c + 1) * P)
                return product3(bank[:, 0:T],
                                lambda i: (w_hi[k][:, i, cols], xT_hi[par][:, i, :]),
                                lambda i: (w_hi[k][:, i, cols], xT_lo[par][:, i, :]),
                                lambda i: (w_lo[k][:, i, cols], xT_hi[par][:, i, :]))

            def project_v(j, par):
                rows = slice(j * P, (j + 1) * P)
                return product3(V_BANK[j][:, 0:H],
                                lambda i: (xT_hi[par][:, i, rows], w_hi["v"][:, i, :]),
                                lambda i: (xT_hi[par][:, i, rows], w_lo["v"][:, i, :]),
                                lambda i: (xT_lo[par][:, i, rows], w_hi["v"][:, i, :]))

            def scores(s, h, par):
                if h % 2 == 0:
                    wait(pe, q_lo_done[h // 2], s + 1)
                    wait(pe, k_twice[h // 2], s + 1)
                    wait(pe, k_lo_done[h // 2], s + 1)
                wait(pe, masked[(h - 2) % HEADS], s + 1 if h >= 2 else s)
                for j in range(J):
                    o = bank_s[h % 2][:, j * T:(j + 1) * T]
                    q = q_stack[par][:, h, j * P:(j + 1) * P]
                    pe.matmul(o, q, k_high2[par][:, h, :], start=True, stop=False)
                    last = pe.matmul(o, q, k_low0[par][:, h, :], start=False, stop=True)
                last.then_inc(s_mm[h], 1)

            def transposes(n, h, par):
                wait(pe, probs_done[h], n + 1)
                wait(pe, probsT_done[(h - 2) % HEADS], n + 1 if h >= 2 else n)
                for kc in range(J):
                    for j in range(J):
                        last = pe.transpose(bank_t[h % 2][:, kc * T + j * P:kc * T + (j + 1) * P],
                                            probs[par][:, h, j, kc * P:(kc + 1) * P], ident[:])
                last.then_inc(t_mm[h], 1)

            def context(n, c, par):
                if c == 0:
                    wait(pe, v_done[J - 1], n + 1)
                wait(pe, probsT_done[2 * c], n + 1)
                wait(pe, probsT_done[2 * c + 1], n + 1)
                wait(pe, ctx_lo_done[(2, 1, 0)[c]], n + 1 if c == 2 else n)
                for kc in range(J):
                    for e in range(2):
                        h = 2 * c + e
                        last = pe.matmul(bank_c[c % 2][e * D:(e + 1) * D, 0:T],
                                         v[par][:, kc, h * D:(h + 1) * D], probsT[:, h, kc, :],
                                         start=(kc == 0), stop=(kc == J - 1))
                last.then_inc(c_mm[c], 1)

            def out_product(n, j, par):
                rows = slice(j * P, (j + 1) * P)
                if j == 0:
                    wait(pe, ctx_lo_done[C - 1], n + 1)
                product3(O_BANK[j][:, 0:H],
                         lambda i: (ctx_hi[par][:, i, rows], w_hi["f"][:, i, :]),
                         lambda i: (ctx_hi[par][:, i, rows], w_lo["f"][:, i, :]),
                         lambda i: (ctx_lo[par][:, i, rows], w_hi["f"][:, i, :])).then_inc(o_mm[j], 1)

            def shift_product():
                pe.wait_ge(bv_rep_done, 1)
                pe.wait_ge(w_in["f"], 16)
                for i in range(C):
                    last = pe.matmul(bank_c[1][:, 0:H], bv_rep[:, i, :], w_raw["f"][:, i, :],
                                     start=(i == 0), stop=(i == C - 1))
                last.then_inc(shift_mm, 1)

            def slot(s, par, after):
                first = isinstance(s, int) and s == -1
                proj, score, attend, outs = (within(s, a) for a in (1, 0, -1, -2))
                old = 1 - par
                for c in range(C):
                    if score:
                        scores(s, 2 * c, par)
                    if proj:
                        if c == 0:
                            wait(pe, x_lo_done, s + 2)
                        if first and c == 0:
                            pe.wait_ge(w_lo_done, 1)
                        if c == 0:
                            wait(pe, v_done[0], s + 1)
                        elif outs:
                            wait(pe, y_done[c - 1], s - 1)
                        else:
                            wait(pe, q_lo_done[c - 1], s + 2)
                        project("q", q_bank(s + 1, c), c, old).then_inc(q_mm[c], 1)
                    if attend:
                        transposes(s - 1, 2 * c, old)
                    if outs and c < J:
                        if proj:
                            wait(pe, (v_done[1], k_lo_done[0])[c], (s + 1, s + 2)[c])
                        elif s == B - 1:
                            wait(pe, v_done[1 - c], B)
                        else:
                            wait(pe, y_done[c], s - 2)
                        if isinstance(s, int) and s == 2:
                            pe.wait_ge(w_lo_done, 4)
                        out_product(s - 2, c, par)
                    if score:
                        scores(s, 2 * c + 1, par)
                    if attend:
                        transposes(s - 1, 2 * c + 1, old)
                    if proj:
                        if first and c == 0:
                            pe.wait_ge(w_lo_done, 2)
                        if outs and c < J:
                            wait(pe, q_lo_done[c], s + 2)
                        elif c > 0:
                            wait(pe, k_lo_done[c - 1], s + 2)
                        else:
                            wait(pe, v_done[1], s + 1)
                        project("k", k_bank(s + 1, c), c, old).then_inc(k_mm[c], 1)
                    if attend:
                        context(s - 1, c, old)
                if proj:
                    if first:
                        pe.wait_ge(w_lo_done, 3)
                    wait(pe, q_lo_done[2], s + 2)
                    project_v(0, old).then_inc(v_mm[0], 1)
                    wait(pe, k_lo_done[2], s + 2)
                    project_v(1, old).then_inc(v_mm[1], 1)
                if first:
                    shift_product()

            pe.wait_ge(small_in, 48)
            slots(pe, slot)

        @block.scalar
        def _(act):
            def high(k):
                act.wait_ge(w_in[k], 16)
                act.copy(w_hi[k][:], w_raw[k][:]).then_inc(w_hi_done, 1)

            def exps(s, h, par):
                wait(act, masked[h], s + 1)
                for j in range(J):
                    e = act.activation(probs[par][:, h, j, :], probs[par][:, h, j, :], ACT.Exp,
                                       bias=least[par][:, h, j:j + 1], scale=-1.0,
                                       accum_out=total[par][:, h, j:j + 1])
                e.then_inc(exp_done[h], 1)

            def q_high(n, c, par):
                wait(act, q_mm[c], n + 1)
                for e in range(2):
                    rows = slice(e * D, (e + 1) * D)
                    a = act.activation(q_stack[par][rows, 2 * c + e, :], q_bank(n, c)[rows, 0:T],
                                       ACT.Identity, bias=bcol[rows, 0, c:c + 1])
                a.then_inc(q_hi_done[c], 1)

            def k_high(n, c, par):
                wait(act, k_mm[c], n + 1)
                for e in range(2):
                    rows = slice(e * D, (e + 1) * D)
                    a = act.activation(k_high2[par][rows, 2 * c + e, :], k_bank(n, c)[rows, 0:T],
                                       ACT.Identity, bias=bcol[rows, 1, c:c + 1])
                a.then_inc(k_hi_done[c], 1)

            def copy_probsT(n, h):
                wait(act, t_mm[h], n + 1)
                wait(act, c_mm[h // 2], n)
                act.copy(probsT[:, h], bank_t[h % 2][:].rearrange("p (k t) -> p k t", k=J)
                         ).then_inc(probsT_done[h], 1)

            def ctx_high(n, c, par):
                wait(act, c_mm[c], n + 1)
                wait(act, o_mm[J - 1], n - 1)
                act.copy(ctx_hi[par][:, c, :], bank_c[c % 2][:, 0:T]).then_inc(ctx_hi_done[c], 1)

            def copy_v(n, j, par):
                wait(act, v_mm[j], n + 1)
                wait(act, c_mm[C - 1], n - 1)
                act.copy(v[par][:, j, :], V_BANK[j][:, 0:H]).then_inc(v_done[j], 1)

            def slot(s, par, after):
                first = isinstance(s, int) and s == -1
                proj, score, attend = (within(s, a) for a in (1, 0, -1))
                old = 1 - par
                for c in range(J):
                    if proj:
                        q_high(s + 1, c, old)
                    if score:
                        exps(s, 2 * c, par)
                    if attend:
                        copy_probsT(s - 1, 2 * c)
                        copy_probsT(s - 1, 2 * c + 1)
                    if proj:
                        k_high(s + 1, c, old)
                    if score:
                        exps(s, 2 * c + 1, par)
                    if attend:
                        ctx_high(s - 1, c, old)
                    if first and c == 0:
                        high("v")
                if proj:
                    q_high(s + 1, 2, old)
                if attend:
                    copy_probsT(s - 1, 4)
                    copy_probsT(s - 1, 5)
                if proj:
                    k_high(s + 1, 2, old)
                if attend:
                    ctx_high(s - 1, 2, old)
                for j in range(J):
                    if score:
                        exps(s, 4 + j, par)
                    if proj:
                        copy_v(s + 1, j, old)
                if first:
                    high("f")

            high("q")
            act.wait_ge(small_in, 48)
            high("k")
            slots(act, slot)

        @block.vector
        def _(dve):
            def low(k, n):
                dve.wait_ge(w_hi_done, n)
                dve.tensor_tensor(w_lo[k][:], w_raw[k][:], w_hi[k][:], ALU.subtract).then_inc(w_lo_done, 1)

            def x_high(n, par):
                dve.wait_ge(xT_in[par], dmas(n, par))
                dve.tensor_copy(xT_hi[par][:], xT_raw[par][:]).then_inc(x_hi_done, 1)

            def make_mask(n, par):
                dve.wait_ge(adj_done_in[par], dmas(n, par))
                dve.tensor_scalar(mask[par][:], adj_in[par][:], 1.0, -NEG / SCALE, ALU.subtract, ALU.mult
                                  ).then_inc(mask_done, 1)

            def mask_scores(after, h, par):
                wait(dve, s_mm[h], after, apart=True)
                if h == 0:
                    wait(dve, mask_done, after)
                for j in range(J):
                    m = dve.tensor_tensor_reduce(probs[par][:, h, j, :], bank_s[h % 2][:, j * T:(j + 1) * T],
                                                 mask[par][:, j, :], -SCALE, LEAST_START, ALU.add, ALU.min,
                                                 least[par][:, h, j:j + 1])
                m.then_inc(masked[h], 1)

            def invert(s, h, par):
                wait(dve, exp_done[h], s + 1)
                dve.reciprocal(inv[par][:, h, :], total[par][:, h, :]).then_inc(inv_done[h], 1)

            def q_low(n, c, par):
                wait(dve, q_hi_done[c], n + 1)
                for e in range(2):
                    rows, other = slice(e * D, (e + 1) * D), slice((1 - e) * D, (2 - e) * D)
                    o = dve.scalar_tensor_tensor(q_stack[par][other, 2 * c + e, :], q_bank(n, c)[rows, 0:T],
                                                 bcol[rows, 0, c:c + 1],
                                                 q_stack[par][rows, 2 * c + e, :].bitcast(F32),
                                                 ALU.add, ALU.subtract)
                o.then_inc(q_lo_done[c], 1)

            def k_low(n, c, par):
                wait(dve, k_hi_done[c], n + 1)
                for e in range(2):
                    rows = slice(e * D, (e + 1) * D)
                    o = dve.scalar_tensor_tensor(k_low0[par][rows, 2 * c + e, :], k_bank(n, c)[rows, 0:T],
                                                 bcol[rows, 1, c:c + 1],
                                                 k_high2[par][rows, 2 * c + e, :].bitcast(F32),
                                                 ALU.add, ALU.subtract)
                o.then_inc(k_lo_done[c], 1)

            def k_copy(c, par):
                for e in range(2):
                    rows, other = slice(e * D, (e + 1) * D), slice((1 - e) * D, (2 - e) * D)
                    o = dve.tensor_copy(k_high2[par][other, 2 * c + e, :], k_high2[par][rows, 2 * c + e, :])
                o.then_inc(k_twice[c], 1)

            def ctx_low(n, c, par):
                wait(dve, ctx_hi_done[c], n + 1)
                dve.tensor_tensor(ctx_lo[par][:, c, :], bank_c[c % 2][:, 0:T], ctx_hi[par][:, c, :].bitcast(F32),
                                  ALU.subtract).then_inc(ctx_lo_done[c], 1)

            def add_resid(n, j, par):
                wait(dve, o_mm[j], n + 1)
                if j == 0:
                    wait(dve, resid_done, n + 1)
                    if not isinstance(n, int) or n >= 2:
                        dve.wait_ge(stored[par], dmas(n - 2, par))
                dve.tensor_tensor(y[par][:, j, :], O_BANK[j][:, 0:H], resid[par][:, j, :], ALU.add
                                  ).then_inc(y_done[j], 1)

            def row_stats(n, j, par):
                wait(dve, y_done[j], n + 1)
                dve.bn_stats(stats[:, j, :], y[par][:, j, :]).then_inc(stats_done[j], 1)

            def mean_and_var(n, j):
                wait(dve, stats_done[j], n + 1, apart=True)
                dve.bn_aggr(mean_var[:, j, :], stats[:, j, :]).then_inc(mean_done[j], 1)

            def add_eps(n, j):
                wait(dve, mean_done[j], n + 1)
                dve.tensor_scalar(var_eps[:, j:j + 1], mean_var[:, j, 1:2], EPS, None, ALU.add
                                  ).then_inc(var_done[j], 1)

            def normalise(n, j, par):
                wait(dve, rstd_done[j], n + 1)
                dve.tensor_scalar(y[par][:, j, :], y[par][:, j, :], mean_var[:, j, 0:1], rstd[:, j:j + 1],
                                  ALU.subtract, ALU.mult).then_inc(normed[j], 1)

            def finish_pair(s, c, old):
                if within(s, 1):
                    k_copy(c, old)
                if within(s, -1):
                    ctx_low(s - 1, c, old)

            def slot(s, par, after):
                first = isinstance(s, int) and s == -1
                proj, score, attend, outs, split = (within(s, a) for a in (1, 0, -1, -2, 2))
                old = 1 - par
                if attend:
                    invert(s - 1, HEADS - 1, old)
                for c in range(C):
                    out_now = outs and c < J
                    if score:
                        mask_scores(after, 2 * c, par)
                    if c > 0:
                        finish_pair(s, c - 1, old)
                        if score:
                            invert(s, 2 * c - 1, par)
                    if proj:
                        q_low(s + 1, c, old)
                    if first and c == 0:
                        low("k", 2)
                    if score and c < 2:
                        invert(s, 2 * c, par)
                    if outs and c == 1:
                        normalise(s - 2, 0, par)
                    if out_now:
                        add_resid(s - 2, c, par)
                    if score:
                        mask_scores(after, 2 * c + 1, par)
                    if out_now:
                        row_stats(s - 2, c, par)
                        mean_and_var(s - 2, c)
                        add_eps(s - 2, c)
                    if proj:
                        k_low(s + 1, c, old)
                    if outs and c == 2:
                        normalise(s - 2, 1, par)
                    if c == 2:
                        if split:
                            x_high(s + 2, par)
                        if proj:
                            make_mask(s + 1, old)
                    if score and c == 2:
                        invert(s, 2 * c, par)
                    if first and c == 0:
                        low("v", 3)
                finish_pair(s, C - 1, old)
                if first:
                    low("f", 4)
                    dve.wait_ge(shift_mm, 1)
                    dve.tensor_tensor(shift[:], bank_c[1][:, 0:H], bf_rows[:], ALU.add).then_inc(shift_done, 1)

            x_high(0, 0)
            low("q", 1)
            dve.wait_ge(small_in, 48)
            dve.tensor_copy(bv_rep[:], bcol[:, 2, :].unsqueeze(2).to_broadcast((P, C, P))
                            ).then_inc(bv_rep_done, 1)
            dve.wait_ge(zeros_done, 2)
            slots(dve, slot)

        @block.gpsimd
        def _(pool):
            def x_low(n, par):
                wait(pool, x_hi_done, n + 1)
                pool.tensor_tensor(xT_lo[par][:], xT_raw[par][:], xT_hi[par][:].bitcast(F32), ALU.subtract
                                   ).then_inc(x_lo_done, 1)

            def add_shift(n, par):
                pool.wait_ge(x_in[par], dmas(n, par))
                pool.tensor_tensor(resid[par][:], resid[par][:],
                                   shift[:].unsqueeze(1).to_broadcast((P, J, H)), ALU.add
                                   ).then_inc(resid_done, 1)

            def divide(s, h, par):
                wait(pool, inv_done[h], s + 1)
                pool.tensor_tensor(probs[par][:, h], probs[par][:, h],
                                   inv[par][:, h, :].unsqueeze(2).to_broadcast((P, J, T)), ALU.mult
                                   ).then_inc(probs_done[h], 1)

            def inv_std(n, j):
                wait(pool, var_done[j], n + 1)
                pool.tensor_tensor(rstd[:, j:j + 1], var_eps[:, j:j + 1], minus_half[:], ALU.pow
                                   ).then_inc(rstd_done[j], 1)

            def slot(s, par, after):
                for h in range(HEADS):
                    if within(s, -2) and h in (1, 3):
                        inv_std(s - 2, h // 2)
                    if within(s, 0):
                        divide(s, h, par)
                    if h == 0 and within(s, -1):
                        if isinstance(s, int) and s == 1:
                            pool.wait_ge(shift_done, 1)
                        add_shift(s - 1, 1 - par)
                    if h == 3 and within(s, 2):
                        x_low(s + 2, par)

            pool.memset(minus_half[:], -0.5).then_inc(half_done, 1)
            for par in range(2):
                pool.memset(k_low0[par][:].bitcast(F32), 0.0).then_inc(zeros_done, 1)
            x_low(0, 0)
            pool.wait_ge(half_done, 1)
            slots(pool, slot)


_SHAPE = (B, T, H)


def kernel(x, adj, L0_gnn_Wq, L0_gnn_bq, L0_gnn_Wk, L0_gnn_bk, L0_gnn_Wv, L0_gnn_bv, L0_gnn_Wf, L0_gnn_bf):
    import concourse.bacc as bacc
    from concourse.bass_utils import run_bass_kernel_spmd

    x = np.asarray(x)
    cols = [np.asarray(b).reshape(C, P).T for b in (L0_gnn_bq, L0_gnn_bk, L0_gnn_bv)]
    arrays = {
        "xT": x.reshape(B, T, C, P).transpose(0, 3, 2, 1),
        "x": x,
        "adj": np.asarray(adj).reshape(B, J, P, T).transpose(0, 2, 1, 3),
        "wq": np.asarray(L0_gnn_Wq), "wk": np.asarray(L0_gnn_Wk),
        "wv": np.asarray(L0_gnn_Wv), "wf": np.asarray(L0_gnn_Wf),
        "bias_cols": np.stack(cols, axis=1),
        "bf": np.asarray(L0_gnn_bf).reshape(1, H),
        "eye": np.eye(P, dtype=np.float32),
    }
    arrays = {k: np.ascontiguousarray(a) for k, a in arrays.items()}
    nc = bacc.Bacc("TRN2", target_bir_lowering=False, num_devices=1)
    args = [nc.dram_tensor(f"{k}_dram", a.shape, mybir.dt.from_np(a.dtype), kind="ExternalInput").ap()
            for k, a in arrays.items()]
    out = nc.dram_tensor("out_dram", _SHAPE, F32, kind="ExternalOutput").ap()
    build(nc, *args, out)
    r = run_bass_kernel_spmd(nc, [{f"{k}_dram": a for k, a in arrays.items()}], core_ids=[0])
    return r.results[0]["out_dram"]
```

```python
from contextlib import ExitStack

import numpy as np

import concourse.bass as bass
from concourse import mybir
from concourse.alu_op_type import AluOpType as ALU

F32 = mybir.dt.float32
F32R = mybir.dt.float32r
BF16 = mybir.dt.bfloat16
U8 = mybir.dt.uint8
ACT = mybir.ActivationFunctionType

P = 128
B, T, H = 32, 256, 384
HEADS = 6
D = H // HEADS
C = H // P
J = T // P
SCALE = 1.0 / float(np.sqrt(D))
NEG = -9000000000000000.0
LEAST_START = 3.0e38
EPS = 1e-5
WARMING = 14
LAST = B + 1
LOOP = (4, 30)
FIRST, OTHERS, ALL = slice(0, P), slice(P, H), slice(0, H)
PARTS = [("q", FIRST), ("k", FIRST), ("q", OTHERS), ("k", OTHERS), ("v", ALL), ("f", ALL)]


def build(nc, xT, x, adj, wq, wk, wv, wf, bias_cols, bf, eye, out):
    with ExitStack() as ctx:
        def sb(name, shape, dt=F32):
            return ctx.enter_context(nc.sbuf_tensor(name, shape, dt))

        def pair(name, shape, dt=F32):
            return [sb(f"{name}{i}", shape, dt) for i in range(2)]

        def bank(name):
            return ctx.enter_context(nc.psum_tensor(name, [P, 512], F32))

        def sem(name):
            return ctx.enter_context(nc.semaphore(name))

        def sems(name, n):
            return [sem(f"{name}{i}") for i in range(n)]

        w_raw = {k: sb(f"w{k}_raw", [P, C, H]) for k in "qkvf"}
        w_hi = {k: sb(f"w{k}_hi", [P, C, H], F32R) for k in "qkvf"}
        w_lo = {k: sb(f"w{k}_lo", [P, C, H], F32R) for k in "qkvf"}
        ident = sb("ident", [P, P])
        bcol = sb("bcol", [P, 3, C])
        bv_rep = sb("bv_rep", [P, C, P])
        bf_rows = sb("bf_rows", [P, H])
        shift = sb("shift", [P, H])

        xT_raw = pair("xT_raw", [P, C, T])
        xT_hi = pair("xT_hi", [P, C, T], F32R)
        xT_lo = pair("xT_lo", [P, C, T], F32R)
        resid = pair("resid", [P, J, H])
        adj_in = pair("adj_in", [P, J, T], U8)
        mask = pair("mask", [P, J, T], BF16)
        q_stack = pair("q_stack", [P, HEADS, T], F32R)
        k_high2 = pair("k_high2", [P, HEADS, T], F32R)
        k_low0 = pair("k_low0", [P, HEADS, T], F32R)
        v = pair("v", [P, J, H])
        probs = pair("probs", [P, HEADS, J, T])
        least = pair("least", [P, HEADS, J])
        total = pair("total", [P, HEADS, J])
        inv = pair("inv", [P, HEADS, J])
        probsT = sb("probsT", [P, HEADS, J, T])
        ctx_hi = pair("ctx_hi", [P, C, T], F32R)
        ctx_lo = pair("ctx_lo", [P, C, T], F32R)
        y = pair("y", [P, J, H])
        stats = sb("stats", [P, J, 6])
        mean_var = sb("mean_var", [P, J, 2])
        var_eps = sb("var_eps", [P, J])
        minus_half = sb("minus_half", [P, 1])
        rstd = sb("rstd", [P, J])

        bank_a, bank_b = bank("bank_a"), bank("bank_b")
        bank_s = [bank(f"bank_s{i}") for i in range(2)]
        bank_t = [bank(f"bank_t{i}") for i in range(2)]
        bank_c = [bank(f"bank_c{i}") for i in range(2)]
        O_BANK, V_BANK = [bank_b, bank_a], [bank_a, bank_b]

        def q_bank(n, c):
            if isinstance(n, int) and n < 2:
                return [bank_a, bank_t[0], bank_c[0]][c]
            return bank_a if isinstance(n, int) and n == 2 else [bank_a, bank_b, bank_a][c]

        def k_bank(n, c):
            if isinstance(n, int) and n < 2:
                return [bank_b, bank_t[1], bank_t[0]][c]
            return bank_b if isinstance(n, int) and n == 2 else [bank_a, bank_b, bank_b][c]

        w_in = sems("w_in", len(PARTS))
        w_hi_done, qk_lo_done, vf_lo_done = sem("w_hi_done"), sem("qk_lo_done"), sem("vf_lo_done")
        small_in = sem("small_in")
        zeros_done, half_done = sem("zeros_done"), sem("half_done")
        bv_rep_done, shift_mm, shift_done = sem("bv_rep_done"), sem("shift_mm"), sem("shift_done")
        xT_in, x_in, adj_done_in = sems("xT_in", 2), sems("x_in", 2), sems("adj_in_done", 2)
        stored = sems("stored", 2)
        q_mm, k_mm, v_mm = sems("q_mm", C), sems("k_mm", C), sems("v_mm", J)
        s_mm, t_mm = sems("s_mm", HEADS), sems("t_mm", HEADS)
        c_mm, o_mm = sems("c_mm", C), sems("o_mm", J)
        q_hi_done, k_hi_done = sems("q_hi_done", C), sems("k_hi_done", C)
        exp_done, probsT_done = sems("exp_done", HEADS), sems("probsT_done", HEADS)
        ctx_hi_done, v_done = sems("ctx_hi_done", C), sems("v_done", J)
        x_hi_done, mask_done = sem("x_hi_done"), sem("mask_done")
        masked = sems("masked", HEADS)
        inv_done = sems("inv_done", HEADS)
        q_lo_done, k_lo_done, k_twice = sems("q_lo_done", C), sems("k_lo_done", C), sems("k_twice", C)
        ctx_lo_done = sems("ctx_lo_done", C)
        y_done, stats_done, mean_done = sems("y_done", J), sems("stats_done", J), sems("mean_done", J)
        var_done, normed = sems("var_done", J), sems("normed", J)
        x_lo_done, resid_done = sem("x_lo_done"), sem("resid_done")
        probs_done = sems("probs_done", HEADS)
        rstd_done = sems("rstd_done", J)

        def wait(engine, semaphore, batches, apart=False):
            if apart and not isinstance(batches, int):
                engine.wait_ge(small_in, 48)
            if not isinstance(batches, int) or batches > 0:
                engine.wait_ge(semaphore, batches)

        def dmas(n, par):
            return n * 8 + (16 - 8 * par)

        def slots(engine, slot, closing_slot):
            for s in range(LOOP[0]):
                slot(s, s % 2, s + 1)
            with engine.Fori(LOOP[0] + 1, LOOP[1], 2) as odd:
                slot(odd - 1, 0, odd)
                slot(odd, 1, odd + 1)
            for s in range(LOOP[1], B - 1):
                slot(s, s % 2, s + 1)
            for s in range(B - 1, LAST + 1):
                closing_slot(s, s % 2)

        def within(s, ahead):
            return not isinstance(s, int) or 0 <= s + ahead < B

        dram = {"q": wq, "k": wk, "v": wv, "f": wf}
        block = ctx.enter_context(nc.Block())

        @block.sync
        def _(sp):
            def load_xT(n, par):
                wait(sp, x_lo_done, n - 1, apart=True)
                sp.dma_start(xT_raw[par][:], xT[bass.ds(n, 1)].rearrange("b p c t -> p (b c) t")
                             ).then_inc(xT_in[par], 16)

            def load_adj(n, par):
                wait(sp, mask_done, n - 1, apart=True)
                sp.dma_start(adj_in[par][:], adj[bass.ds(n, 1)].rearrange("b p j t -> p (b j) t")
                             ).then_inc(adj_done_in[par], 16)

            def load_w(i):
                k, cols = PARTS[i]
                sp.dma_start(w_raw[k][:, :, cols], dram[k].rearrange("(c p) n -> p c n", p=P)[:, :, cols]
                             ).then_inc(w_in[i], 16)

            def slot(s, par, after):
                if within(s, 2):
                    load_xT(s + 2, par)
                    load_adj(s + 2, par)
                if within(s, 0):
                    wait(sp, y_done[J - 1], s - 1, apart=True)
                    sp.dma_start(resid[par][:], x[bass.ds(s, 1)].rearrange("b (j p) d -> p (b j) d", p=P)
                                 ).then_inc(x_in[par], 16)
                if within(s, -2):
                    wait(sp, normed[J - 1], s - 1, apart=True)
                    sp.dma_start(out[bass.ds(s - 2, 1)].rearrange("b (j p) d -> p (b j) d", p=P), y[par][:]
                                 ).then_inc(stored[par], 16)

            load_w(0)
            load_xT(0, 0)
            load_w(1)
            sp.dma_start(bcol[:], bias_cols).then_inc(small_in, 16)
            load_w(2)
            load_w(3)
            sp.dma_start(ident[:], eye).then_inc(small_in, 16)
            sp.dma_start(bf_rows[:], bf.to_broadcast((P, H))).then_inc(small_in, 16)
            load_w(4)
            load_xT(1, 1)
            load_adj(0, 0)
            load_w(5)
            load_adj(1, 1)
            slots(sp, slot, lambda s, par: slot(s, par, s + 1))
            for par in range(2):
                sp.wait_ge(stored[par], 16 * (B // 2))

        @block.tensor
        def _(pe):
            def product3(o, hi_hi, hi_lo, lo_hi):
                ops = [f(c) for c in range(C) for f in (hi_hi, hi_lo, lo_hi)]
                for i, (stationary, moving) in enumerate(ops):
                    last = pe.matmul(o, stationary, moving, start=(i == 0), stop=(i == len(ops) - 1))
                return last

            def project(k, bank, c, par):
                cols = slice(c * P, (c + 1) * P)
                return product3(bank[:, 0:T],
                                lambda i: (w_hi[k][:, i, cols], xT_hi[par][:, i, :]),
                                lambda i: (w_hi[k][:, i, cols], xT_lo[par][:, i, :]),
                                lambda i: (w_lo[k][:, i, cols], xT_hi[par][:, i, :]))

            def project_v(j, par):
                rows = slice(j * P, (j + 1) * P)
                return product3(V_BANK[j][:, 0:H],
                                lambda i: (xT_hi[par][:, i, rows], w_hi["v"][:, i, :]),
                                lambda i: (xT_hi[par][:, i, rows], w_lo["v"][:, i, :]),
                                lambda i: (xT_lo[par][:, i, rows], w_hi["v"][:, i, :]))

            def scores(s, h, par):
                if h % 2 == 0:
                    wait(pe, q_lo_done[h // 2], s + 1)
                    wait(pe, k_twice[h // 2], s + 1)
                    wait(pe, k_lo_done[h // 2], s + 1)
                wait(pe, masked[(h - 2) % HEADS], s + 1 if h >= 2 else s)
                for j in range(J):
                    o = bank_s[h % 2][:, j * T:(j + 1) * T]
                    q = q_stack[par][:, h, j * P:(j + 1) * P]
                    pe.matmul(o, q, k_high2[par][:, h, :], start=True, stop=False)
                    last = pe.matmul(o, q, k_low0[par][:, h, :], start=False, stop=True)
                last.then_inc(s_mm[h], 1)

            def transposes(n, h, par):
                wait(pe, probs_done[h], n + 1)
                wait(pe, probsT_done[(h - 2) % HEADS], n + 1 if h >= 2 else n)
                for kc in range(J):
                    for j in range(J):
                        last = pe.transpose(bank_t[h % 2][:, kc * T + j * P:kc * T + (j + 1) * P],
                                            probs[par][:, h, j, kc * P:(kc + 1) * P], ident[:])
                last.then_inc(t_mm[h], 1)

            def context(n, c, par):
                if c == 0:
                    wait(pe, v_done[J - 1], n + 1)
                wait(pe, probsT_done[2 * c], n + 1)
                wait(pe, probsT_done[2 * c + 1], n + 1)
                wait(pe, ctx_lo_done[(2, 1, 0)[c]], n + 1 if c == 2 else n)
                for kc in range(J):
                    for e in range(2):
                        h = 2 * c + e
                        last = pe.matmul(bank_c[c % 2][e * D:(e + 1) * D, 0:T],
                                         v[par][:, kc, h * D:(h + 1) * D], probsT[:, h, kc, :],
                                         start=(kc == 0), stop=(kc == J - 1))
                last.then_inc(c_mm[c], 1)

            def out_product(n, j, par):
                rows = slice(j * P, (j + 1) * P)
                if j == 0:
                    wait(pe, ctx_lo_done[C - 1], n + 1)
                product3(O_BANK[j][:, 0:H],
                         lambda i: (ctx_hi[par][:, i, rows], w_hi["f"][:, i, :]),
                         lambda i: (ctx_hi[par][:, i, rows], w_lo["f"][:, i, :]),
                         lambda i: (ctx_lo[par][:, i, rows], w_hi["f"][:, i, :])).then_inc(o_mm[j], 1)

            def shift_product():
                pe.wait_ge(bv_rep_done, 1)
                pe.wait_ge(w_in[5], 16)
                for i in range(C):
                    last = pe.matmul(bank_c[1][:, 0:H], bv_rep[:, i, :], w_raw["f"][:, i, :],
                                     start=(i == 0), stop=(i == C - 1))
                last.then_inc(shift_mm, 1)

            def opening():
                pe.wait_ge(zeros_done, 1)
                for i in range(WARMING):
                    pe.matmul(bank_s[0][:, 0:T], k_low0[0][:, 0, 0:P], k_low0[0][:, 0, :], start=True, stop=True)
                pe.wait_ge(w_hi_done, 1)
                pe.wait_ge(x_hi_done, 1)
                o = q_bank(0, 0)[:, 0:T]
                for i in range(C):
                    pe.matmul(o, w_hi["q"][:, i, FIRST], xT_hi[0][:, i, :], start=(i == 0), stop=False)
                pe.wait_ge(qk_lo_done, 1)
                for i in range(C):
                    pe.matmul(o, w_lo["q"][:, i, FIRST], xT_hi[0][:, i, :], start=False, stop=False)
                pe.wait_ge(x_lo_done, 1)
                for i in range(C):
                    last = pe.matmul(o, w_hi["q"][:, i, FIRST], xT_lo[0][:, i, :], start=False, stop=(i == C - 1))
                last.then_inc(q_mm[0], 1)
                pe.wait_ge(qk_lo_done, 2)
                project("k", k_bank(0, 0), 0, 0).then_inc(k_mm[0], 1)
                for c in range(1, C):
                    if c == 1:
                        pe.wait_ge(qk_lo_done, 3)
                    project("q", q_bank(0, c), c, 0).then_inc(q_mm[c], 1)
                    if c == 1:
                        pe.wait_ge(qk_lo_done, 4)
                    if c == 2:
                        pe.wait_ge(q_lo_done[1], 1)
                    project("k", k_bank(0, c), c, 0).then_inc(k_mm[c], 1)
                products_v(-1, 0)

            def products_v(s, par):
                spread = isinstance(s, int) and s < 1
                if isinstance(s, int) and s == -1:
                    pe.wait_ge(vf_lo_done, 1)
                wait(pe, q_lo_done[0 if spread else 2], s + 2)
                project_v(0, par).then_inc(v_mm[0], 1)
                wait(pe, k_lo_done[0 if spread else 2], s + 2)
                project_v(1, par).then_inc(v_mm[1], 1)

            def slot(s, par, after):
                score, attend, outs = (within(s, a) for a in (0, -1, -2))
                old = 1 - par
                for c in range(C):
                    scores(s, 2 * c, par)
                    if c == 0:
                        wait(pe, x_lo_done, s + 2)
                    if c == 0:
                        wait(pe, v_done[0], s + 1)
                    elif outs:
                        wait(pe, y_done[c - 1], s - 1)
                    elif attend:
                        wait(pe, q_lo_done[c - 1], s + 2)
                    elif c == 1:
                        wait(pe, k_lo_done[2], s + 1)
                    else:
                        wait(pe, q_lo_done[2], s + 1)
                    project("q", q_bank(s + 1, c), c, old).then_inc(q_mm[c], 1)
                    if attend:
                        if c == 0 and not outs:
                            wait(pe, k_lo_done[2], s + 1)
                        transposes(s - 1, 2 * c, old)
                    if outs and c < J:
                        wait(pe, (v_done[1], k_lo_done[0])[c], (s + 1, s + 2)[c])
                        if isinstance(s, int) and s == 2 and c == 0:
                            pe.wait_ge(vf_lo_done, 2)
                        out_product(s - 2, c, par)
                    scores(s, 2 * c + 1, par)
                    if attend:
                        transposes(s - 1, 2 * c + 1, old)
                    if outs and c < J:
                        wait(pe, q_lo_done[c], s + 2)
                    elif c == 0:
                        wait(pe, v_done[1], s + 1)
                    elif attend:
                        wait(pe, k_lo_done[c - 1], s + 2)
                    elif c == 1:
                        wait(pe, k_lo_done[1], s + 1)
                    else:
                        wait(pe, q_lo_done[1], s + 2)
                    project("k", k_bank(s + 1, c), c, old).then_inc(k_mm[c], 1)
                    if attend:
                        context(s - 1, c, old)
                if not attend:
                    shift_product()
                products_v(s, old)

            def closing_slot(s, par):
                score, attend, outs = (within(s, a) for a in (0, -1, -2))
                old = 1 - par
                for c in range(C):
                    for h in (2 * c, 2 * c + 1):
                        if score:
                            scores(s, h, par)
                        if attend:
                            transposes(s - 1, h, old)
                    if c == 0:
                        if s == B - 1:
                            wait(pe, v_done[1], B)
                        else:
                            wait(pe, y_done[0], s - 2)
                        out_product(s - 2, 0, par)
                    elif attend:
                        context(s - 1, c - 1, old)
                if attend:
                    context(s - 1, C - 1, old)
                if s == B - 1:
                    wait(pe, v_done[0], B)
                else:
                    wait(pe, y_done[1], s - 2)
                out_product(s - 2, 1, par)

            opening()
            pe.wait_ge(small_in, 48)
            slots(pe, slot, closing_slot)

        @block.scalar
        def _(act):
            def high(i):
                k, cols = PARTS[i]
                act.wait_ge(w_in[i], 16)
                act.copy(w_hi[k][:, :, cols], w_raw[k][:, :, cols]).then_inc(w_hi_done, 1)

            def exps(s, h, par):
                wait(act, masked[h], s + 1)
                for j in range(J):
                    e = act.activation(probs[par][:, h, j, :], probs[par][:, h, j, :], ACT.Exp,
                                       bias=least[par][:, h, j:j + 1], scale=-1.0,
                                       accum_out=total[par][:, h, j:j + 1])
                e.then_inc(exp_done[h], 1)

            def q_high(n, c, par):
                wait(act, q_mm[c], n + 1)
                for e in range(2):
                    rows = slice(e * D, (e + 1) * D)
                    a = act.activation(q_stack[par][rows, 2 * c + e, :], q_bank(n, c)[rows, 0:T],
                                       ACT.Identity, bias=bcol[rows, 0, c:c + 1])
                a.then_inc(q_hi_done[c], 1)

            def k_high(n, c, par):
                wait(act, k_mm[c], n + 1)
                for e in range(2):
                    rows = slice(e * D, (e + 1) * D)
                    a = act.activation(k_high2[par][rows, 2 * c + e, :], k_bank(n, c)[rows, 0:T],
                                       ACT.Identity, bias=bcol[rows, 1, c:c + 1])
                a.then_inc(k_hi_done[c], 1)

            def copy_probsT(n, h):
                wait(act, t_mm[h], n + 1)
                wait(act, c_mm[h // 2], n)
                act.copy(probsT[:, h], bank_t[h % 2][:].rearrange("p (k t) -> p k t", k=J)
                         ).then_inc(probsT_done[h], 1)

            def ctx_high(n, c, par):
                wait(act, c_mm[c], n + 1)
                wait(act, o_mm[J - 1], n - 1)
                act.copy(ctx_hi[par][:, c, :], bank_c[c % 2][:, 0:T]).then_inc(ctx_hi_done[c], 1)

            def copy_v(n, j, par):
                wait(act, v_mm[j], n + 1)
                wait(act, c_mm[C - 1], n - 1)
                act.copy(v[par][:, j, :], V_BANK[j][:, 0:H]).then_inc(v_done[j], 1)

            def opening():
                high(0)
                high(1)
                act.wait_ge(small_in, 48)
                q_high(0, 0, 0)
                high(2)
                k_high(0, 0, 0)
                high(3)
                q_high(0, 1, 0)
                k_high(0, 1, 0)
                high(4)
                q_high(0, 2, 0)
                k_high(0, 2, 0)
                high(5)
                for j in range(J):
                    copy_v(0, j, 0)

            def slot(s, par, after):
                attend = within(s, -1)
                old = 1 - par
                for c in range(J):
                    q_high(s + 1, c, old)
                    exps(s, 2 * c, par)
                    if attend:
                        copy_probsT(s - 1, 2 * c)
                        copy_probsT(s - 1, 2 * c + 1)
                    k_high(s + 1, c, old)
                    exps(s, 2 * c + 1, par)
                    if attend:
                        ctx_high(s - 1, c, old)
                q_high(s + 1, 2, old)
                if attend:
                    copy_probsT(s - 1, 4)
                    copy_probsT(s - 1, 5)
                k_high(s + 1, 2, old)
                if attend:
                    ctx_high(s - 1, 2, old)
                for j in range(J):
                    exps(s, 4 + j, par)
                    copy_v(s + 1, j, old)

            def closing_slot(s, par):
                score, attend = within(s, 0), within(s, -1)
                for c in range(C):
                    for h in (2 * c, 2 * c + 1):
                        if score:
                            exps(s, h, par)
                        if attend:
                            copy_probsT(s - 1, h)
                    if attend and c > 0:
                        ctx_high(s - 1, c - 1, 1 - par)
                if attend:
                    ctx_high(s - 1, C - 1, 1 - par)

            opening()
            slots(act, slot, closing_slot)

        @block.vector
        def _(dve):
            def low(i):
                k, cols = PARTS[i]
                dve.wait_ge(w_hi_done, i + 1)
                dve.tensor_tensor(w_lo[k][:, :, cols], w_raw[k][:, :, cols], w_hi[k][:, :, cols].bitcast(F32),
                                  ALU.subtract).then_inc(qk_lo_done, 1)

            def x_high(n, par):
                dve.wait_ge(xT_in[par], dmas(n, par))
                dve.tensor_copy(xT_hi[par][:], xT_raw[par][:]).then_inc(x_hi_done, 1)

            def make_mask(n, par):
                dve.wait_ge(adj_done_in[par], dmas(n, par))
                dve.tensor_scalar(mask[par][:], adj_in[par][:], 1.0, -NEG / SCALE, ALU.subtract, ALU.mult
                                  ).then_inc(mask_done, 1)

            def mask_scores(after, h, par):
                wait(dve, s_mm[h], after, apart=True)
                if h == 0:
                    wait(dve, mask_done, after)
                for j in range(J):
                    m = dve.tensor_tensor_reduce(probs[par][:, h, j, :], bank_s[h % 2][:, j * T:(j + 1) * T],
                                                 mask[par][:, j, :], -SCALE, LEAST_START, ALU.add, ALU.min,
                                                 least[par][:, h, j:j + 1])
                m.then_inc(masked[h], 1)

            def invert(s, h, par):
                wait(dve, exp_done[h], s + 1)
                dve.reciprocal(inv[par][:, h, :], total[par][:, h, :]).then_inc(inv_done[h], 1)

            def q_low(n, c, par):
                wait(dve, q_hi_done[c], n + 1)
                for e in range(2):
                    rows, other = slice(e * D, (e + 1) * D), slice((1 - e) * D, (2 - e) * D)
                    o = dve.scalar_tensor_tensor(q_stack[par][other, 2 * c + e, :], q_bank(n, c)[rows, 0:T],
                                                 bcol[rows, 0, c:c + 1],
                                                 q_stack[par][rows, 2 * c + e, :].bitcast(F32),
                                                 ALU.add, ALU.subtract)
                o.then_inc(q_lo_done[c], 1)

            def k_low(n, c, par):
                wait(dve, k_hi_done[c], n + 1)
                for e in range(2):
                    rows = slice(e * D, (e + 1) * D)
                    o = dve.scalar_tensor_tensor(k_low0[par][rows, 2 * c + e, :], k_bank(n, c)[rows, 0:T],
                                                 bcol[rows, 1, c:c + 1],
                                                 k_high2[par][rows, 2 * c + e, :].bitcast(F32),
                                                 ALU.add, ALU.subtract)
                o.then_inc(k_lo_done[c], 1)

            def k_copy(c, par):
                for e in range(2):
                    rows, other = slice(e * D, (e + 1) * D), slice((1 - e) * D, (2 - e) * D)
                    o = dve.tensor_copy(k_high2[par][other, 2 * c + e, :], k_high2[par][rows, 2 * c + e, :])
                o.then_inc(k_twice[c], 1)

            def ctx_low(n, c, par):
                wait(dve, ctx_hi_done[c], n + 1)
                dve.tensor_tensor(ctx_lo[par][:, c, :], bank_c[c % 2][:, 0:T], ctx_hi[par][:, c, :].bitcast(F32),
                                  ALU.subtract).then_inc(ctx_lo_done[c], 1)

            def add_resid(n, j, par):
                wait(dve, o_mm[j], n + 1)
                if j == 0:
                    wait(dve, resid_done, n + 1)
                    if not isinstance(n, int) or n >= 2:
                        dve.wait_ge(stored[par], dmas(n - 2, par))
                dve.tensor_tensor(y[par][:, j, :], O_BANK[j][:, 0:H], resid[par][:, j, :], ALU.add
                                  ).then_inc(y_done[j], 1)

            def row_stats(n, j, par):
                wait(dve, y_done[j], n + 1)
                dve.bn_stats(stats[:, j, :], y[par][:, j, :]).then_inc(stats_done[j], 1)

            def mean_and_var(n, j):
                wait(dve, stats_done[j], n + 1, apart=True)
                dve.bn_aggr(mean_var[:, j, :], stats[:, j, :]).then_inc(mean_done[j], 1)

            def add_eps(n, j):
                wait(dve, mean_done[j], n + 1)
                dve.tensor_scalar(var_eps[:, j:j + 1], mean_var[:, j, 1:2], EPS, None, ALU.add
                                  ).then_inc(var_done[j], 1)

            def normalise(n, j, par):
                wait(dve, rstd_done[j], n + 1)
                dve.tensor_scalar(y[par][:, j, :], y[par][:, j, :], mean_var[:, j, 0:1], rstd[:, j:j + 1],
                                  ALU.subtract, ALU.mult).then_inc(normed[j], 1)

            def finish_pair(s, c, old):
                k_copy(c, old)
                if within(s, -1):
                    ctx_low(s - 1, c, old)

            def layer_norm(n, j, par):
                row_stats(n, j, par)
                mean_and_var(n, j)
                add_eps(n, j)

            def opening():
                x_high(0, 0)
                low(0)
                dve.wait_ge(x_hi_done, 1)
                dve.tensor_tensor(xT_lo[0][:], xT_raw[0][:], xT_hi[0][:].bitcast(F32), ALU.subtract
                                  ).then_inc(x_lo_done, 1)
                low(1)
                dve.wait_ge(small_in, 48)
                dve.tensor_copy(bv_rep[:], bcol[:, 2, :].unsqueeze(2).to_broadcast((P, C, P))
                                ).then_inc(bv_rep_done, 1)
                dve.wait_ge(zeros_done, 2)
                q_low(0, 0, 0)
                low(2)
                k_low(0, 0, 0)
                low(3)
                k_copy(0, 0)
                q_low(0, 1, 0)
                k_low(0, 1, 0)
                k_copy(1, 0)
                x_high(1, 1)
                q_low(0, 2, 0)
                k_low(0, 2, 0)
                make_mask(0, 0)
                k_copy(2, 0)

            def slot(s, par, after):
                attend, outs = within(s, -1), within(s, -2)
                old = 1 - par
                if attend:
                    invert(s - 1, HEADS - 1, old)
                for c in range(C):
                    out_now = outs and c < J
                    mask_scores(after, 2 * c, par)
                    if c == 0 and within(s, 2):
                        x_high(s + 2, par)
                    if c > 0:
                        finish_pair(s, c - 1, old)
                        invert(s, 2 * c - 1, par)
                    q_low(s + 1, c, old)
                    if c < 2:
                        invert(s, 2 * c, par)
                    if outs and c == 1:
                        normalise(s - 2, 0, par)
                    if out_now:
                        add_resid(s - 2, c, par)
                    mask_scores(after, 2 * c + 1, par)
                    if out_now:
                        layer_norm(s - 2, c, par)
                    k_low(s + 1, c, old)
                    if outs and c == 2:
                        normalise(s - 2, 1, par)
                    if c == 2:
                        make_mask(s + 1, old)
                        invert(s, 2 * c, par)
                finish_pair(s, C - 1, old)
                if not attend:
                    dve.wait_ge(shift_mm, 1)
                    dve.tensor_tensor(shift[:], bank_c[1][:, 0:H], bf_rows[:], ALU.add).then_inc(shift_done, 1)

            def closing_slot(s, par):
                score, attend = within(s, 0), within(s, -1)
                old = 1 - par
                if attend:
                    invert(s - 1, HEADS - 1, old)
                for c in range(C):
                    if score:
                        mask_scores(s + 1, 2 * c, par)
                        if c > 0:
                            invert(s, 2 * c - 1, par)
                        mask_scores(s + 1, 2 * c + 1, par)
                        invert(s, 2 * c, par)
                    if c == 0:
                        add_resid(s - 2, 0, par)
                        layer_norm(s - 2, 0, par)
                    elif attend:
                        ctx_low(s - 1, c - 1, old)
                        if c == 1:
                            normalise(s - 2, 0, par)
                if attend:
                    ctx_low(s - 1, C - 1, old)
                add_resid(s - 2, 1, par)
                layer_norm(s - 2, 1, par)
                if not attend:
                    normalise(s - 2, 0, par)
                normalise(s - 2, 1, par)

            opening()
            slots(dve, slot, closing_slot)

        @block.gpsimd
        def _(pool):
            def x_low(n, par):
                wait(pool, x_hi_done, n + 1)
                pool.tensor_tensor(xT_lo[par][:], xT_raw[par][:], xT_hi[par][:].bitcast(F32), ALU.subtract
                                   ).then_inc(x_lo_done, 1)

            def low(i):
                k, cols = PARTS[i]
                pool.wait_ge(w_hi_done, i + 1)
                pool.tensor_tensor(w_lo[k][:, :, cols], w_raw[k][:, :, cols], w_hi[k][:, :, cols].bitcast(F32),
                                   ALU.subtract).then_inc(vf_lo_done, 1)

            def add_shift(n, par):
                pool.wait_ge(x_in[par], dmas(n, par))
                pool.tensor_tensor(resid[par][:], resid[par][:],
                                   shift[:].unsqueeze(1).to_broadcast((P, J, H)), ALU.add
                                   ).then_inc(resid_done, 1)

            def divide(s, h, par):
                wait(pool, inv_done[h], s + 1)
                pool.tensor_tensor(probs[par][:, h], probs[par][:, h],
                                   inv[par][:, h, :].unsqueeze(2).to_broadcast((P, J, T)), ALU.mult
                                   ).then_inc(probs_done[h], 1)

            def inv_std(n, j):
                wait(pool, var_done[j], n + 1)
                pool.tensor_tensor(rstd[:, j:j + 1], var_eps[:, j:j + 1], minus_half[:], ALU.pow
                                   ).then_inc(rstd_done[j], 1)

            def slot(s, par, after):
                if within(s, -1):
                    divide(s - 1, HEADS - 1, 1 - par)
                for h in range(HEADS - 1):
                    if within(s, -2) and h in (1, 3):
                        inv_std(s - 2, h // 2)
                    divide(s, h, par)
                    if h == 0 and within(s, -1):
                        if isinstance(s, int) and s == 1:
                            pool.wait_ge(shift_done, 1)
                        add_shift(s - 1, 1 - par)
                    if h == 2 and within(s, 2):
                        x_low(s + 2, par)

            def closing_slot(s, par):
                if within(s, -1):
                    divide(s - 1, HEADS - 1, 1 - par)
                    add_shift(s - 1, 1 - par)
                for h in range(HEADS - 1):
                    if within(s, 0):
                        divide(s, h, par)
                    if h == 1:
                        inv_std(s - 2, 0)
                inv_std(s - 2, 1)

            pool.memset(minus_half[:], -0.5).then_inc(half_done, 1)
            for par in range(2):
                pool.memset(k_low0[par][:].bitcast(F32), 0.0).then_inc(zeros_done, 1)
            pool.wait_ge(half_done, 1)
            low(4)
            x_low(1, 1)
            low(5)
            slots(pool, slot, closing_slot)


_SHAPE = (B, T, H)


def kernel(x, adj, L0_gnn_Wq, L0_gnn_bq, L0_gnn_Wk, L0_gnn_bk, L0_gnn_Wv, L0_gnn_bv, L0_gnn_Wf, L0_gnn_bf):
    import concourse.bacc as bacc
    from concourse.bass_utils import run_bass_kernel_spmd

    x = np.asarray(x)
    cols = [np.asarray(b).reshape(C, P).T for b in (L0_gnn_bq, L0_gnn_bk, L0_gnn_bv)]
    arrays = {
        "xT": x.reshape(B, T, C, P).transpose(0, 3, 2, 1),
        "x": x,
        "adj": np.asarray(adj).reshape(B, J, P, T).transpose(0, 2, 1, 3),
        "wq": np.asarray(L0_gnn_Wq), "wk": np.asarray(L0_gnn_Wk),
        "wv": np.asarray(L0_gnn_Wv), "wf": np.asarray(L0_gnn_Wf),
        "bias_cols": np.stack(cols, axis=1),
        "bf": np.asarray(L0_gnn_bf).reshape(1, H),
        "eye": np.eye(P, dtype=np.float32),
    }
    arrays = {k: np.ascontiguousarray(a) for k, a in arrays.items()}
    nc = bacc.Bacc("TRN2", target_bir_lowering=False, num_devices=1)
    args = [nc.dram_tensor(f"{k}_dram", a.shape, mybir.dt.from_np(a.dtype), kind="ExternalInput").ap()
            for k, a in arrays.items()]
    out = nc.dram_tensor("out_dram", _SHAPE, F32, kind="ExternalOutput").ap()
    build(nc, *args, out)
    r = run_bass_kernel_spmd(nc, [{f"{k}_dram": a for k, a in arrays.items()}], core_ids=[0])
    return r.results[0]["out_dram"]
```

```python
from contextlib import ExitStack

import numpy as np

import concourse.bass as bass
from concourse import mybir
from concourse.alu_op_type import AluOpType as ALU

F32 = mybir.dt.float32
F32R = mybir.dt.float32r
U8 = mybir.dt.uint8
ACT = mybir.ActivationFunctionType

P = 128
B, T, H = 32, 256, 384
HEADS = 6
D = H // HEADS
C = H // P
J = T // P
SCALE = 1.0 / float(np.sqrt(D))
NEG = -9000000000000000.0
LEAST_START = 3.0e38
EPS = 1e-5
WARMING = 12
LAST = B + 1
LOOP = (4, 30)
FIRST, OTHERS, ALL = slice(0, P), slice(P, H), slice(0, H)
PARTS = [("q", FIRST), ("k", FIRST), ("q", OTHERS), ("k", OTHERS), ("v", ALL), ("f", ALL)]


def build(nc, xT, x, adj, wq, wk, wv, wf, bias_cols, bf, eye, out):
    with ExitStack() as ctx:
        def sb(name, shape, dt=F32):
            return ctx.enter_context(nc.sbuf_tensor(name, shape, dt))

        def pair(name, shape, dt=F32):
            return [sb(f"{name}{i}", shape, dt) for i in range(2)]

        def bank(name):
            return ctx.enter_context(nc.psum_tensor(name, [P, 512], F32))

        def sem(name):
            return ctx.enter_context(nc.semaphore(name))

        def sems(name, n):
            return [sem(f"{name}{i}") for i in range(n)]

        w_raw = {k: sb(f"w{k}_raw", [P, C, H]) for k in "qkvf"}
        w_hi = {k: sb(f"w{k}_hi", [P, C, H], F32R) for k in "qkvf"}
        w_lo = {k: sb(f"w{k}_lo", [P, C, H], F32R) for k in "qkvf"}
        ident = sb("ident", [P, P])
        bcol = sb("bcol", [P, 3, C])
        bv_rep = sb("bv_rep", [P, C, P])
        bf_rows = sb("bf_rows", [P, H])
        shift = sb("shift", [P, H])

        xT_raw = pair("xT_raw", [P, C, T])
        xT_hi = pair("xT_hi", [P, C, T], F32R)
        xT_lo = pair("xT_lo", [P, C, T], F32R)
        resid = pair("resid", [P, J, H])
        adj_in = pair("adj_in", [P, J, T], U8)
        mask = pair("mask", [P, J, T])
        q_stack = pair("q_stack", [P, HEADS, T], F32R)
        k_high2 = pair("k_high2", [P, HEADS, T], F32R)
        k_low0 = pair("k_low0", [P, HEADS, T], F32R)
        v = pair("v", [P, J, H])
        probs = pair("probs", [P, HEADS, J, T])
        least = pair("least", [P, HEADS, J])
        total = pair("total", [P, HEADS, J])
        inv = pair("inv", [P, HEADS, J])
        probsT = sb("probsT", [P, HEADS, J, T])
        ctx_hi = pair("ctx_hi", [P, C, T], F32R)
        ctx_lo = pair("ctx_lo", [P, C, T], F32R)
        y = pair("y", [P, J, H])
        stats = sb("stats", [P, J, 6])
        mean_var = sb("mean_var", [P, J, 2])
        var_eps = sb("var_eps", [P, J])
        minus_half = sb("minus_half", [P, 1])
        rstd = sb("rstd", [P, J])

        bank_a, bank_b = bank("bank_a"), bank("bank_b")
        bank_s = [bank(f"bank_s{i}") for i in range(2)]
        bank_t = [bank(f"bank_t{i}") for i in range(2)]
        bank_c = [bank(f"bank_c{i}") for i in range(2)]
        O_BANK, V_BANK = [bank_b, bank_a], [bank_a, bank_b]

        def q_bank(n, c):
            if isinstance(n, int) and n < 2:
                return [bank_a, bank_t[0], bank_c[0]][c]
            return bank_a if isinstance(n, int) and n == 2 else [bank_a, bank_b, bank_a][c]

        def k_bank(n, c):
            if isinstance(n, int) and n < 2:
                return [bank_b, bank_t[1], bank_t[0] if n else bank_s[1]][c]
            return bank_b if isinstance(n, int) and n == 2 else [bank_a, bank_b, bank_b][c]

        w_in = sems("w_in", len(PARTS))
        w_hi_done, qk_lo_done, vf_lo_done = sem("w_hi_done"), sem("qk_lo_done"), sem("vf_lo_done")
        bcol_in = sem("bcol_in")
        small_in = sem("small_in")
        zeros_done, half_done = sem("zeros_done"), sem("half_done")
        bv_rep_done, shift_mm, shift_done = sem("bv_rep_done"), sem("shift_mm"), sem("shift_done")
        xT_in, x_in, adj_arrived = sems("xT_in", 2), sems("x_in", 2), sems("adj_arrived", 2)
        stored = sems("stored", 2)
        q_mm, k_mm, v_mm = sems("q_mm", C), sems("k_mm", C), sems("v_mm", J)
        s_mm, t_mm = sems("s_mm", HEADS), sems("t_mm", HEADS)
        c_mm, o_mm = sems("c_mm", C), sems("o_mm", J)
        q_hi_done, k_hi_done = sems("q_hi_done", C), sems("k_hi_done", C)
        exp_done, probsT_done = sems("exp_done", HEADS), sems("probsT_done", HEADS)
        ctx_hi_done, v_done = sems("ctx_hi_done", C), sems("v_done", J)
        x_hi_done, mask_done = sem("x_hi_done"), sem("mask_done")
        masked = sems("masked", HEADS)
        inv_done = sems("inv_done", HEADS)
        q_lo_done, k_lo_done, k_twice = sems("q_lo_done", C), sems("k_lo_done", C), sems("k_twice", C)
        ctx_lo_done = sems("ctx_lo_done", C)
        y_done, stats_done, mean_done = sems("y_done", J), sems("stats_done", J), sems("mean_done", J)
        var_done, normed = sems("var_done", J), sems("normed", J)
        x_lo_done, resid_done = sem("x_lo_done"), sem("resid_done")
        probs_done = sems("probs_done", HEADS)
        rstd_done = sems("rstd_done", J)

        def wait(engine, semaphore, batches, apart=False):
            if apart and not isinstance(batches, int):
                engine.wait_ge(small_in, 32)
            if not isinstance(batches, int) or batches > 0:
                engine.wait_ge(semaphore, batches)

        def dmas(n, par):
            return n * 8 + (16 - 8 * par)

        def slots(engine, slot, closing_slot):
            for s in range(LOOP[0]):
                slot(s, s % 2, s + 1)
            with engine.Fori(LOOP[0] + 1, LOOP[1], 2) as odd:
                slot(odd - 1, 0, odd)
                slot(odd, 1, odd + 1)
            for s in range(LOOP[1], B - 1):
                slot(s, s % 2, s + 1)
            for s in range(B - 1, LAST + 1):
                closing_slot(s, s % 2)

        def within(s, ahead):
            return not isinstance(s, int) or 0 <= s + ahead < B

        dram = {"q": wq, "k": wk, "v": wv, "f": wf}
        block = ctx.enter_context(nc.Block())

        @block.sync
        def _(sp):
            def load_xT(n, par):
                wait(sp, x_lo_done, n - 1, apart=True)
                sp.dma_start(xT_raw[par][:], xT[bass.ds(n, 1)].rearrange("b p c t -> p (b c) t")
                             ).then_inc(xT_in[par], 16)

            def load_adj(n, par):
                wait(sp, mask_done, n - 1, apart=True)
                sp.dma_start(adj_in[par][:], adj[bass.ds(n, 1)].rearrange("b p j t -> p (b j) t")
                             ).then_inc(adj_arrived[par], 16)

            def load_w(i):
                k, cols = PARTS[i]
                sp.dma_start(w_raw[k][:, :, cols], dram[k].rearrange("(c p) n -> p c n", p=P)[:, :, cols]
                             ).then_inc(w_in[i], 16)

            def slot(s, par, after):
                if within(s, 2):
                    load_xT(s + 2, par)
                    load_adj(s + 2, par)
                if within(s, 0):
                    wait(sp, y_done[J - 1], s - 1, apart=True)
                    sp.dma_start(resid[par][:], x[bass.ds(s, 1)].rearrange("b (j p) d -> p (b j) d", p=P)
                                 ).then_inc(x_in[par], 16)
                if within(s, -2):
                    wait(sp, normed[J - 1], s - 1, apart=True)
                    sp.dma_start(out[bass.ds(s - 2, 1)].rearrange("b (j p) d -> p (b j) d", p=P), y[par][:]
                                 ).then_inc(stored[par], 16)

            load_w(0)
            load_xT(0, 0)
            load_w(1)
            sp.dma_start(bcol[:], bias_cols).then_inc(bcol_in, 16)
            load_w(2)
            load_w(3)
            sp.dma_start(ident[:], eye).then_inc(small_in, 16)
            sp.dma_start(bf_rows[:], bf.to_broadcast((P, H))).then_inc(small_in, 16)
            load_w(4)
            load_xT(1, 1)
            load_adj(0, 0)
            load_w(5)
            load_adj(1, 1)
            slots(sp, slot, lambda s, par: slot(s, par, s + 1))
            for par in range(2):
                sp.wait_ge(stored[par], 16 * (B // 2))

        @block.tensor
        def _(pe):
            def product3(o, *three, gates=None):
                ops = ([(i, c) for c in range(C) for i in range(3)] if gates is None else
                       [(i, c) for i in range(3) for c in range(C)])
                for n, (i, c) in enumerate(ops):
                    if gates is not None and c == 0:
                        pe.wait_ge(*gates[i])
                    last = pe.matmul(o, *three[i](c), start=(n == 0), stop=(n == len(ops) - 1))
                return last

            def project(k, bank, c, par, gates=None):
                cols = slice(c * P, (c + 1) * P)
                return product3(bank[:, 0:T],
                                lambda i: (w_hi[k][:, i, cols], xT_hi[par][:, i, :]),
                                lambda i: (w_lo[k][:, i, cols], xT_hi[par][:, i, :]),
                                lambda i: (w_hi[k][:, i, cols], xT_lo[par][:, i, :]), gates=gates)

            def project_v(j, par, gates=None):
                rows = slice(j * P, (j + 1) * P)
                return product3(V_BANK[j][:, 0:H],
                                lambda i: (xT_hi[par][:, i, rows], w_hi["v"][:, i, :]),
                                lambda i: (xT_lo[par][:, i, rows], w_hi["v"][:, i, :]),
                                lambda i: (xT_hi[par][:, i, rows], w_lo["v"][:, i, :]), gates=gates)

            def scores(s, h, par):
                if h % 2 == 0:
                    wait(pe, q_lo_done[h // 2], s + 1)
                    wait(pe, k_twice[h // 2], s + 1)
                    wait(pe, k_lo_done[h // 2], s + 1)
                wait(pe, masked[(h - 2) % HEADS], s + 1 if h >= 2 else s)
                for j in range(J):
                    o = bank_s[h % 2][:, j * T:(j + 1) * T]
                    q = q_stack[par][:, h, j * P:(j + 1) * P]
                    pe.matmul(o, q, k_high2[par][:, h, :], start=True, stop=False)
                    last = pe.matmul(o, q, k_low0[par][:, h, :], start=False, stop=True)
                last.then_inc(s_mm[h], 1)

            def transposes(n, h, par):
                wait(pe, probs_done[h], n + 1)
                wait(pe, probsT_done[(h - 2) % HEADS], n + 1 if h >= 2 else n)
                for kc in range(J):
                    for j in range(J):
                        last = pe.transpose(bank_t[h % 2][:, kc * T + j * P:kc * T + (j + 1) * P],
                                            probs[par][:, h, j, kc * P:(kc + 1) * P], ident[:])
                last.then_inc(t_mm[h], 1)

            def context(n, c, par):
                if c == 0:
                    wait(pe, v_done[J - 1], n + 1)
                wait(pe, probsT_done[2 * c], n + 1)
                wait(pe, probsT_done[2 * c + 1], n + 1)
                wait(pe, ctx_lo_done[(2, 1, 0)[c]], n + 1 if c == 2 else n)
                for kc in range(J):
                    for e in range(2):
                        h = 2 * c + e
                        last = pe.matmul(bank_c[c % 2][e * D:(e + 1) * D, 0:T],
                                         v[par][:, kc, h * D:(h + 1) * D], probsT[:, h, kc, :],
                                         start=(kc == 0), stop=(kc == J - 1))
                last.then_inc(c_mm[c], 1)

            def out_product(n, j, par):
                rows = slice(j * P, (j + 1) * P)
                if j == 0:
                    wait(pe, ctx_lo_done[C - 1], n + 1)
                product3(O_BANK[j][:, 0:H],
                         lambda i: (ctx_hi[par][:, i, rows], w_hi["f"][:, i, :]),
                         lambda i: (ctx_hi[par][:, i, rows], w_lo["f"][:, i, :]),
                         lambda i: (ctx_lo[par][:, i, rows], w_hi["f"][:, i, :])).then_inc(o_mm[j], 1)

            def shift_product():
                pe.wait_ge(bv_rep_done, 1)
                pe.wait_ge(w_in[5], 16)
                for i in range(C):
                    last = pe.matmul(bank_c[1][:, 0:H], bv_rep[:, i, :], w_raw["f"][:, i, :],
                                     start=(i == 0), stop=(i == C - 1))
                last.then_inc(shift_mm, 1)

            def opening():
                pe.wait_ge(zeros_done, 1)
                for i in range(WARMING):
                    pe.matmul(bank_s[0][:, 0:T], k_low0[0][:, 0, 0:P], k_low0[0][:, 0, :], start=True, stop=True)
                pe.wait_ge(w_hi_done, 1)
                project("q", q_bank(0, 0), 0, 0, gates=[(x_hi_done, 1), (qk_lo_done, 1), (x_lo_done, 1)]
                        ).then_inc(q_mm[0], 1)
                pe.wait_ge(qk_lo_done, 2)
                project("k", k_bank(0, 0), 0, 0).then_inc(k_mm[0], 1)
                for c in range(1, C):
                    if c == 1:
                        pe.wait_ge(qk_lo_done, 3)
                    project("q", q_bank(0, c), c, 0).then_inc(q_mm[c], 1)
                    if c == 1:
                        pe.wait_ge(qk_lo_done, 4)
                    project("k", k_bank(0, c), c, 0).then_inc(k_mm[c], 1)
                pe.wait_ge(q_lo_done[0], 1)
                project_v(0, 0, gates=[(w_hi_done, 5), (x_lo_done, 1), (vf_lo_done, 1)]).then_inc(v_mm[0], 1)
                pe.wait_ge(k_lo_done[0], 1)
                project_v(1, 0).then_inc(v_mm[1], 1)

            def slot(s, par, after):
                attend, outs = within(s, -1), within(s, -2)
                old = 1 - par
                for c in range(C):
                    scores(s, 2 * c, par)
                    if c == 0:
                        wait(pe, x_lo_done, s + 2)
                    if c == 0:
                        wait(pe, v_done[0], s + 1)
                    elif outs:
                        wait(pe, y_done[c - 1], s - 1)
                    elif attend:
                        wait(pe, q_lo_done[c - 1], s + 2)
                    else:
                        wait(pe, q_lo_done[c], s + 1)
                    project("q", q_bank(s + 1, c), c, old).then_inc(q_mm[c], 1)
                    if attend:
                        if c == 0 and not outs:
                            wait(pe, k_lo_done[2], s + 1)
                        transposes(s - 1, 2 * c, old)
                    if outs and c < J:
                        wait(pe, (v_done[1], k_lo_done[0])[c], (s + 1, s + 2)[c])
                        if isinstance(s, int) and s == 2 and c == 0:
                            pe.wait_ge(vf_lo_done, 2)
                        out_product(s - 2, c, par)
                    if c == 0 and not attend:
                        pe.wait_ge(k_lo_done[2], 1)
                    scores(s, 2 * c + 1, par)
                    if attend:
                        transposes(s - 1, 2 * c + 1, old)
                    if outs and c < J:
                        wait(pe, q_lo_done[c], s + 2)
                    elif c == 0:
                        wait(pe, v_done[1], s + 1)
                    elif attend:
                        wait(pe, k_lo_done[c - 1], s + 2)
                    elif c == 1:
                        wait(pe, k_lo_done[1], s + 1)
                    else:
                        wait(pe, q_lo_done[1], s + 2)
                    project("k", k_bank(s + 1, c), c, old).then_inc(k_mm[c], 1)
                    if attend:
                        context(s - 1, c, old)
                if not attend:
                    shift_product()
                wait(pe, q_lo_done[2 if attend else 0], s + 2)
                project_v(0, old).then_inc(v_mm[0], 1)
                wait(pe, k_lo_done[2 if attend else 0], s + 2)
                project_v(1, old).then_inc(v_mm[1], 1)

            def closing_slot(s, par):
                score, attend = within(s, 0), within(s, -1)
                old = 1 - par
                for c in range(C):
                    for h in (2 * c, 2 * c + 1):
                        if score:
                            scores(s, h, par)
                        if attend:
                            transposes(s - 1, h, old)
                    if c == 0:
                        if s == B - 1:
                            wait(pe, v_done[1], B)
                        else:
                            wait(pe, y_done[0], s - 2)
                        out_product(s - 2, 0, par)
                    elif attend:
                        context(s - 1, c - 1, old)
                if s == B:
                    context(s - 1, C - 1, old)
                if s == B - 1:
                    wait(pe, v_done[0], B)
                else:
                    wait(pe, y_done[1], s - 2)
                out_product(s - 2, 1, par)
                if s == B - 1:
                    context(s - 1, C - 1, old)

            opening()
            pe.wait_ge(small_in, 32)
            slots(pe, slot, closing_slot)

        @block.scalar
        def _(act):
            def high(i):
                k, cols = PARTS[i]
                act.wait_ge(w_in[i], 16)
                act.copy(w_hi[k][:, :, cols], w_raw[k][:, :, cols]).then_inc(w_hi_done, 1)

            def exps(s, h, par):
                wait(act, masked[h], s + 1)
                for j in range(J):
                    e = act.activation(probs[par][:, h, j, :], probs[par][:, h, j, :], ACT.Exp,
                                       bias=least[par][:, h, j:j + 1], scale=-1.0,
                                       accum_out=total[par][:, h, j:j + 1])
                e.then_inc(exp_done[h], 1)

            def q_high(n, c, par):
                wait(act, q_mm[c], n + 1)
                for e in range(2):
                    rows = slice(e * D, (e + 1) * D)
                    a = act.activation(q_stack[par][rows, 2 * c + e, :], q_bank(n, c)[rows, 0:T],
                                       ACT.Identity, bias=bcol[rows, 0, c:c + 1])
                a.then_inc(q_hi_done[c], 1)

            def k_high(n, c, par):
                wait(act, k_mm[c], n + 1)
                for e in range(2):
                    rows = slice(e * D, (e + 1) * D)
                    a = act.activation(k_high2[par][rows, 2 * c + e, :], k_bank(n, c)[rows, 0:T],
                                       ACT.Identity, bias=bcol[rows, 1, c:c + 1])
                a.then_inc(k_hi_done[c], 1)

            def copy_probsT(n, h):
                wait(act, t_mm[h], n + 1)
                wait(act, c_mm[h // 2], n)
                act.copy(probsT[:, h], bank_t[h % 2][:].rearrange("p (k t) -> p k t", k=J)
                         ).then_inc(probsT_done[h], 1)

            def ctx_high(n, c, par):
                wait(act, c_mm[c], n + 1)
                wait(act, o_mm[J - 1], n - 1)
                act.copy(ctx_hi[par][:, c, :], bank_c[c % 2][:, 0:T]).then_inc(ctx_hi_done[c], 1)

            def copy_v(n, j, par):
                wait(act, v_mm[j], n + 1)
                wait(act, c_mm[C - 1], n - 1)
                act.copy(v[par][:, j, :], V_BANK[j][:, 0:H]).then_inc(v_done[j], 1)

            def opening():
                for i in range(4):
                    high(i)
                act.wait_ge(bcol_in, 16)
                q_high(0, 0, 0)
                k_high(0, 0, 0)
                high(4)
                q_high(0, 1, 0)
                k_high(0, 1, 0)
                q_high(0, 2, 0)
                k_high(0, 2, 0)
                high(5)
                for j in range(J):
                    copy_v(0, j, 0)

            def slot(s, par, after):
                attend, outs = within(s, -1), within(s, -2)
                old = 1 - par
                for c in range(J):
                    q_high(s + 1, c, old)
                    if outs or not attend:
                        exps(s, 2 * c, par)
                    if attend:
                        copy_probsT(s - 1, 2 * c)
                        copy_probsT(s - 1, 2 * c + 1)
                    if attend and not outs:
                        exps(s, 2 * c, par)
                    k_high(s + 1, c, old)
                    exps(s, 2 * c + 1, par)
                    if attend:
                        ctx_high(s - 1, c, old)
                q_high(s + 1, 2, old)
                if attend:
                    copy_probsT(s - 1, 4)
                    copy_probsT(s - 1, 5)
                k_high(s + 1, 2, old)
                if attend:
                    ctx_high(s - 1, 2, old)
                for j in range(J):
                    exps(s, 4 + j, par)
                    copy_v(s + 1, j, old)

            def closing_slot(s, par):
                score, attend = within(s, 0), within(s, -1)
                for c in range(C):
                    for h in (2 * c, 2 * c + 1):
                        if score:
                            exps(s, h, par)
                        if attend:
                            copy_probsT(s - 1, h)
                    if attend and c > 0:
                        ctx_high(s - 1, c - 1, 1 - par)
                if attend:
                    ctx_high(s - 1, C - 1, 1 - par)

            opening()
            slots(act, slot, closing_slot)

        @block.vector
        def _(dve):
            def low(i):
                k, cols = PARTS[i]
                dve.wait_ge(w_hi_done, i + 1)
                dve.tensor_tensor(w_lo[k][:, :, cols], w_raw[k][:, :, cols], w_hi[k][:, :, cols].bitcast(F32),
                                  ALU.subtract).then_inc(qk_lo_done, 1)

            def x_high(n, par):
                dve.wait_ge(xT_in[par], dmas(n, par))
                dve.tensor_copy(xT_hi[par][:], xT_raw[par][:]).then_inc(x_hi_done, 1)

            def make_mask(n, par):
                dve.wait_ge(adj_arrived[par], dmas(n, par))
                dve.tensor_scalar(mask[par][:], adj_in[par][:], 1.0, -NEG / SCALE, ALU.subtract, ALU.mult
                                  ).then_inc(mask_done, 1)

            def mask_scores(after, h, par):
                wait(dve, s_mm[h], after, apart=True)
                if h == 0:
                    wait(dve, mask_done, after)
                for j in range(J):
                    m = dve.tensor_tensor_reduce(probs[par][:, h, j, :], bank_s[h % 2][:, j * T:(j + 1) * T],
                                                 mask[par][:, j, :], -SCALE, LEAST_START, ALU.add, ALU.min,
                                                 least[par][:, h, j:j + 1])
                m.then_inc(masked[h], 1)

            def invert(s, h, par):
                wait(dve, exp_done[h], s + 1)
                dve.reciprocal(inv[par][:, h, :], total[par][:, h, :]).then_inc(inv_done[h], 1)

            def q_low(n, c, par):
                wait(dve, q_hi_done[c], n + 1)
                for e in range(2):
                    rows, other = slice(e * D, (e + 1) * D), slice((1 - e) * D, (2 - e) * D)
                    o = dve.scalar_tensor_tensor(q_stack[par][other, 2 * c + e, :], q_bank(n, c)[rows, 0:T],
                                                 bcol[rows, 0, c:c + 1],
                                                 q_stack[par][rows, 2 * c + e, :].bitcast(F32),
                                                 ALU.add, ALU.subtract)
                o.then_inc(q_lo_done[c], 1)

            def k_low(n, c, par):
                wait(dve, k_hi_done[c], n + 1)
                for e in range(2):
                    rows = slice(e * D, (e + 1) * D)
                    o = dve.scalar_tensor_tensor(k_low0[par][rows, 2 * c + e, :], k_bank(n, c)[rows, 0:T],
                                                 bcol[rows, 1, c:c + 1],
                                                 k_high2[par][rows, 2 * c + e, :].bitcast(F32),
                                                 ALU.add, ALU.subtract)
                o.then_inc(k_lo_done[c], 1)

            def k_copy(c, par):
                for e in range(2):
                    rows, other = slice(e * D, (e + 1) * D), slice((1 - e) * D, (2 - e) * D)
                    o = dve.tensor_copy(k_high2[par][other, 2 * c + e, :], k_high2[par][rows, 2 * c + e, :])
                o.then_inc(k_twice[c], 1)

            def ctx_low(n, c, par):
                wait(dve, ctx_hi_done[c], n + 1)
                dve.tensor_tensor(ctx_lo[par][:, c, :], bank_c[c % 2][:, 0:T], ctx_hi[par][:, c, :].bitcast(F32),
                                  ALU.subtract).then_inc(ctx_lo_done[c], 1)

            def add_resid(n, j, par):
                wait(dve, o_mm[j], n + 1)
                if j == 0:
                    wait(dve, resid_done, n + 1)
                    if not isinstance(n, int) or n >= 2:
                        dve.wait_ge(stored[par], dmas(n - 2, par))
                dve.tensor_tensor(y[par][:, j, :], O_BANK[j][:, 0:H], resid[par][:, j, :], ALU.add
                                  ).then_inc(y_done[j], 1)

            def row_stats(n, j, par):
                wait(dve, y_done[j], n + 1)
                dve.bn_stats(stats[:, j, :], y[par][:, j, :]).then_inc(stats_done[j], 1)

            def mean_and_var(n, j):
                wait(dve, stats_done[j], n + 1, apart=True)
                dve.bn_aggr(mean_var[:, j, :], stats[:, j, :]).then_inc(mean_done[j], 1)

            def add_eps(n, j):
                wait(dve, mean_done[j], n + 1)
                dve.tensor_scalar(var_eps[:, j:j + 1], mean_var[:, j, 1:2], EPS, None, ALU.add
                                  ).then_inc(var_done[j], 1)

            def normalise(n, j, par):
                wait(dve, rstd_done[j], n + 1)
                dve.tensor_scalar(y[par][:, j, :], y[par][:, j, :], mean_var[:, j, 0:1], rstd[:, j:j + 1],
                                  ALU.subtract, ALU.mult).then_inc(normed[j], 1)

            def finish_pair(s, c, old):
                k_copy(c, old)
                if within(s, -1):
                    ctx_low(s - 1, c, old)

            def layer_norm(n, j, par):
                row_stats(n, j, par)
                mean_and_var(n, j)
                add_eps(n, j)

            def opening():
                x_high(0, 0)
                low(0)
                dve.wait_ge(x_hi_done, 1)
                dve.tensor_tensor(xT_lo[0][:], xT_raw[0][:], xT_hi[0][:].bitcast(F32), ALU.subtract
                                  ).then_inc(x_lo_done, 1)
                for i in range(1, 4):
                    low(i)
                dve.wait_ge(zeros_done, 2)
                q_low(0, 0, 0)
                k_low(0, 0, 0)
                k_copy(0, 0)
                q_low(0, 1, 0)
                k_low(0, 1, 0)
                k_copy(1, 0)
                x_high(1, 1)
                q_low(0, 2, 0)
                k_low(0, 2, 0)
                make_mask(0, 0)
                k_copy(2, 0)
                dve.tensor_copy(bv_rep[:], bcol[:, 2, :].unsqueeze(2).to_broadcast((P, C, P))
                                ).then_inc(bv_rep_done, 1)

            def slot(s, par, after):
                attend, outs = within(s, -1), within(s, -2)
                old = 1 - par
                if attend:
                    invert(s - 1, HEADS - 1, old)
                for c in range(C):
                    out_now = outs and c < J
                    mask_scores(after, 2 * c, par)
                    if c == 0 and within(s, 2):
                        x_high(s + 2, par)
                    if c > 0:
                        finish_pair(s, c - 1, old)
                        invert(s, 2 * c - 1, par)
                    q_low(s + 1, c, old)
                    if c < 2:
                        invert(s, 2 * c, par)
                    if outs and c == 1:
                        normalise(s - 2, 0, par)
                    if out_now:
                        add_resid(s - 2, c, par)
                    mask_scores(after, 2 * c + 1, par)
                    if out_now:
                        layer_norm(s - 2, c, par)
                    k_low(s + 1, c, old)
                    if outs and c == 2:
                        normalise(s - 2, 1, par)
                    if c == 2:
                        make_mask(s + 1, old)
                        invert(s, 2 * c, par)
                finish_pair(s, C - 1, old)
                if not attend:
                    dve.wait_ge(shift_mm, 1)
                    dve.tensor_tensor(shift[:], bank_c[1][:, 0:H], bf_rows[:], ALU.add).then_inc(shift_done, 1)

            def closing_slot(s, par):
                old = 1 - par
                if s == B - 1:
                    invert(s - 1, HEADS - 1, old)
                    for h in range(HEADS):
                        mask_scores(s + 1, h, par)
                        if h > 0:
                            invert(s, h - 1, par)
                        if h == 3:
                            add_resid(s - 2, 0, par)
                            layer_norm(s - 2, 0, par)
                        if h == 4:
                            ctx_low(s - 1, 0, old)
                    normalise(s - 2, 0, par)
                    ctx_low(s - 1, 1, old)
                    invert(s, HEADS - 1, par)
                    add_resid(s - 2, 1, par)
                    row_stats(s - 2, 1, par)
                    ctx_low(s - 1, 2, old)
                    mean_and_var(s - 2, 1)
                    add_eps(s - 2, 1)
                elif s == B:
                    add_resid(s - 2, 0, par)
                    layer_norm(s - 2, 0, par)
                    normalise(s - 3, 1, old)
                    ctx_low(s - 1, 0, old)
                    normalise(s - 2, 0, par)
                    ctx_low(s - 1, 1, old)
                    ctx_low(s - 1, 2, old)
                    add_resid(s - 2, 1, par)
                    layer_norm(s - 2, 1, par)
                else:
                    add_resid(s - 2, 0, par)
                    row_stats(s - 2, 0, par)
                    normalise(s - 3, 1, old)
                    mean_and_var(s - 2, 0)
                    add_eps(s - 2, 0)
                    add_resid(s - 2, 1, par)
                    layer_norm(s - 2, 1, par)
                    for j in range(J):
                        normalise(s - 2, j, par)

            opening()
            slots(dve, slot, closing_slot)

        @block.gpsimd
        def _(pool):
            def x_low(n, par):
                wait(pool, x_hi_done, n + 1)
                pool.tensor_tensor(xT_lo[par][:], xT_raw[par][:], xT_hi[par][:].bitcast(F32), ALU.subtract
                                   ).then_inc(x_lo_done, 1)

            def low(i):
                k, cols = PARTS[i]
                pool.wait_ge(w_hi_done, i + 1)
                pool.tensor_tensor(w_lo[k][:, :, cols], w_raw[k][:, :, cols], w_hi[k][:, :, cols].bitcast(F32),
                                   ALU.subtract).then_inc(vf_lo_done, 1)

            def add_shift(n, par):
                pool.wait_ge(x_in[par], dmas(n, par))
                pool.tensor_tensor(resid[par][:], resid[par][:],
                                   shift[:].unsqueeze(1).to_broadcast((P, J, H)), ALU.add
                                   ).then_inc(resid_done, 1)

            def divide(s, h, par):
                wait(pool, inv_done[h], s + 1)
                pool.tensor_tensor(probs[par][:, h], probs[par][:, h],
                                   inv[par][:, h, :].unsqueeze(2).to_broadcast((P, J, T)), ALU.mult
                                   ).then_inc(probs_done[h], 1)

            def inv_std(n, j):
                wait(pool, var_done[j], n + 1)
                pool.tensor_tensor(rstd[:, j:j + 1], var_eps[:, j:j + 1], minus_half[:], ALU.pow
                                   ).then_inc(rstd_done[j], 1)

            def slot(s, par, after):
                if within(s, -1):
                    divide(s - 1, HEADS - 1, 1 - par)
                for h in range(HEADS - 1):
                    if within(s, -2) and h in (1, 3):
                        inv_std(s - 2, h // 2)
                    divide(s, h, par)
                    if h == 0 and within(s, -1):
                        if isinstance(s, int) and s == 1:
                            pool.wait_ge(shift_done, 1)
                        add_shift(s - 1, 1 - par)
                    if h == 2 and within(s, 2):
                        x_low(s + 2, par)

            def closing_slot(s, par):
                if within(s, -1):
                    divide(s - 1, HEADS - 1, 1 - par)
                    add_shift(s - 1, 1 - par)
                for h in range(HEADS - 1):
                    if within(s, 0):
                        divide(s, h, par)
                    if h == 1:
                        inv_std(s - 2, 0)
                inv_std(s - 2, 1)

            pool.memset(minus_half[:], -0.5).then_inc(half_done, 1)
            for par in range(2):
                pool.memset(k_low0[par][:].bitcast(F32), 0.0).then_inc(zeros_done, 1)
            pool.wait_ge(half_done, 1)
            low(4)
            x_low(1, 1)
            low(5)
            slots(pool, slot, closing_slot)


_SHAPE = (B, T, H)


def kernel(x, adj, L0_gnn_Wq, L0_gnn_bq, L0_gnn_Wk, L0_gnn_bk, L0_gnn_Wv, L0_gnn_bv, L0_gnn_Wf, L0_gnn_bf):
    import concourse.bacc as bacc
    from concourse.bass_utils import run_bass_kernel_spmd

    x = np.asarray(x)
    cols = [np.asarray(b).reshape(C, P).T for b in (L0_gnn_bq, L0_gnn_bk, L0_gnn_bv)]
    arrays = {
        "xT": x.reshape(B, T, C, P).transpose(0, 3, 2, 1),
        "x": x,
        "adj": np.asarray(adj).reshape(B, J, P, T).transpose(0, 2, 1, 3),
        "wq": np.asarray(L0_gnn_Wq), "wk": np.asarray(L0_gnn_Wk),
        "wv": np.asarray(L0_gnn_Wv), "wf": np.asarray(L0_gnn_Wf),
        "bias_cols": np.stack(cols, axis=1),
        "bf": np.asarray(L0_gnn_bf).reshape(1, H),
        "eye": np.eye(P, dtype=np.float32),
    }
    arrays = {k: np.ascontiguousarray(a) for k, a in arrays.items()}
    nc = bacc.Bacc("TRN2", target_bir_lowering=False, num_devices=1)
    args = [nc.dram_tensor(f"{k}_dram", a.shape, mybir.dt.from_np(a.dtype), kind="ExternalInput").ap()
            for k, a in arrays.items()]
    out = nc.dram_tensor("out_dram", _SHAPE, F32, kind="ExternalOutput").ap()
    build(nc, *args, out)
    r = run_bass_kernel_spmd(nc, [{f"{k}_dram": a for k, a in arrays.items()}], core_ids=[0])
    return r.results[0]["out_dram"]
```
